# Optimizing a Trainium2 kernel written in Bass

```python
import numpy as np
import jax
import jax.numpy as jnp

def _softmax(x, axis=-1):
    return jax.nn.softmax(x, axis=axis)

def _gelu(x):
    return jax.nn.gelu(x, approximate=True)

def _silu(x):
    return jax.nn.silu(x)

def _sigmoid(x):
    return jax.nn.sigmoid(x)

def _layernorm(x, axis=-1, eps=1e-05):
    m = jnp.mean(x, axis=axis, keepdims=True)
    v = jnp.var(x, axis=axis, keepdims=True)
    return (x - m) / jnp.sqrt(v + eps)

def _scatter_add(tgt, idx, src, axis=0):
    return tgt.at[idx].add(src)

def _segment_sum(src, seg, n):
    return jax.ops.segment_sum(src, seg, n)
kernel_name = 'mk_macaron_d1_jaxref_r8_6ddb93'

def setup_inputs(seed: int=0):
    np.random.seed(seed)
    _w = jnp.asarray

    def _L0_attn_setup():
        import jax, jax.numpy as jnp
        import numpy as np
        from jax import lax
        H, KVH, D, CHUNK = (32, 8, 128, 128)
        ROPE_THETA = 10000.0
        RMS_EPS = 1e-05

        def _rope_tables(L):
            inv_freq = 1.0 / ROPE_THETA ** (jnp.arange(0, D, 2, dtype=jnp.float32) / D)
            ang = jnp.arange(L, dtype=jnp.float32)[:, None] * inv_freq
            cos = jnp.concatenate([jnp.cos(ang), jnp.cos(ang)], axis=-1)[:, None, :]
            sin = jnp.concatenate([jnp.sin(ang), jnp.sin(ang)], axis=-1)[:, None, :]
            return (cos, sin)

        def _apply_rope(x, cos, sin):
            half = D // 2
            rot = jnp.concatenate([-x[..., half:], x[..., :half]], axis=-1)
            return x * cos + rot * sin
        key = jax.random.key(seed)
        ks = jax.random.split(key, 10)
        B, L, HID = (1, 512, 512)
        s = lambda fan: 1.0 / np.sqrt(fan)
        return {'hidden_states': jax.random.normal(ks[0], (B, L, HID), jnp.float32), 'Wq': jax.random.normal(ks[1], (H * D, HID), jnp.float32) * s(HID), 'Wk': jax.random.normal(ks[2], (KVH * D, HID), jnp.float32) * s(HID), 'Wv': jax.random.normal(ks[3], (KVH * D, HID), jnp.float32) * s(HID), 'Wo': jax.random.normal(ks[4], (HID, H * D), jnp.float32) * s(H * D), 'Wg': jax.random.normal(ks[5], (H * D, HID), jnp.float32) * (s(HID) * 2 ** (-2.5)), 'Win': jax.random.normal(ks[6], (H, HID), jnp.float32) * s(HID), 'dt_bias': jnp.zeros((H,), jnp.float32), 'A_log_bias': jnp.log(jax.random.uniform(ks[7], (H,), jnp.float32, 1.0, 16.0)), 'gnorm_w': jnp.ones((D,), jnp.float32)}
    _L0_attn_in = _L0_attn_setup()

    def _L0_ffn_setup():
        import jax, jax.numpy as jnp
        import numpy as np
        EPS = 1e-05

        def _bitlinear(x, w):
            scale = jnp.mean(jnp.abs(w))
            q = jnp.round(jnp.clip(w / (scale + EPS), -1.0, 1.0))
            deq = q * scale
            return x @ deq.T
        key = jax.random.key(seed)
        k1, k2, k3, k4 = jax.random.split(key, 4)
        B, S, H, I = (4, 256, 512, 1376)
        return {'hidden_states': jax.random.normal(k1, (B, S, H), dtype=jnp.float32), 'w_gate': jax.random.normal(k2, (I, H), dtype=jnp.float32) * 0.02, 'w_up': jax.random.normal(k3, (I, H), dtype=jnp.float32) * 0.02, 'w_down': jax.random.normal(k4, (H, I), dtype=jnp.float32) * 0.02}
    _L0_ffn_in = _L0_ffn_setup()
    _d = {'L0_attn_hidden_states': _L0_attn_in['hidden_states'], 'L0_attn_Wq': _L0_attn_in['Wq'], 'L0_attn_Wk': _L0_attn_in['Wk'], 'L0_attn_Wv': _L0_attn_in['Wv'], 'L0_attn_Wo': _L0_attn_in['Wo'], 'L0_attn_Wg': _L0_attn_in['Wg'], 'L0_attn_Win': _L0_attn_in['Win'], 'L0_attn_dt_bias': _L0_attn_in['dt_bias'], 'L0_attn_A_log_bias': _L0_attn_in['A_log_bias'], 'L0_attn_gnorm_w': _L0_attn_in['gnorm_w'], 'L0_ffn_w_gate': _L0_ffn_in['w_gate'], 'L0_ffn_w_up': _L0_ffn_in['w_up'], 'L0_ffn_w_down': _L0_ffn_in['w_down']}
    _x0 = _d['L0_attn_hidden_states']
    _d['L0_attn_hidden_states'] = jax.random.normal(jax.random.fold_in(jax.random.key(seed), 1), (4, 256, 512), dtype=_x0.dtype)
    del _x0
    return _d

def reference(L0_attn_hidden_states, L0_attn_Wq, L0_attn_Wk, L0_attn_Wv, L0_attn_Wo, L0_attn_Wg, L0_attn_Win, L0_attn_dt_bias, L0_attn_A_log_bias, L0_attn_gnorm_w, L0_ffn_w_gate, L0_ffn_w_up, L0_ffn_w_down):

    def _L0_attn_ref(hidden_states, Wq, Wk, Wv, Wo, Wg, Win, dt_bias, A_log_bias, gnorm_w):
        import jax, jax.numpy as jnp
        import numpy as np
        from jax import lax
        H, KVH, D, CHUNK = (32, 8, 128, 128)
        ROPE_THETA = 10000.0
        RMS_EPS = 1e-05

        def _rope_tables(L):
            inv_freq = 1.0 / ROPE_THETA ** (jnp.arange(0, D, 2, dtype=jnp.float32) / D)
            ang = jnp.arange(L, dtype=jnp.float32)[:, None] * inv_freq
            cos = jnp.concatenate([jnp.cos(ang), jnp.cos(ang)], axis=-1)[:, None, :]
            sin = jnp.concatenate([jnp.sin(ang), jnp.sin(ang)], axis=-1)[:, None, :]
            return (cos, sin)

        def _apply_rope(x, cos, sin):
            half = D // 2
            rot = jnp.concatenate([-x[..., half:], x[..., :half]], axis=-1)
            return x * cos + rot * sin
        B, L, HID = hidden_states.shape
        NC = L // CHUNK
        q = (hidden_states @ Wq.T).reshape(B, L, H, D)
        k = (hidden_states @ Wk.T).reshape(B, L, KVH, D)
        v = (hidden_states @ Wv.T).reshape(B, L, KVH, D)
        cos, sin = _rope_tables(L)
        q = _apply_rope(q, cos, sin)
        k = _apply_rope(k, cos, sin)
        k = jnp.repeat(k, H // KVH, axis=2)
        v = jnp.repeat(v, H // KVH, axis=2)
        dt = jax.nn.softplus(hidden_states @ Win.T + dt_bias)
        A = -jnp.exp(A_log_bias)
        g = dt * A

        def chunked(t):
            return t.transpose(0, 2, 1, 3).reshape(B, H, NC, CHUNK, D)
        qc, kc = (chunked(q), chunked(k))
        xc = chunked(v * dt[..., None])
        gc = g.transpose(0, 2, 1).reshape(B, H, NC, CHUNK)
        G = jnp.cumsum(gc, axis=-1)
        scores = jnp.einsum('bhnid,bhnjd->bhnij', qc, kc)
        idx = jnp.arange(CHUNK)
        causal = idx[:, None] >= idx[None, :]
        decay = jnp.where(causal, jnp.exp(G[..., :, None] - G[..., None, :]), 0.0)
        y_intra = jnp.einsum('bhnij,bhnjd->bhnid', scores * decay, xc)
        Glast = G[..., -1:]
        k_dec = kc * jnp.exp(Glast - G)[..., None]
        cstates = jnp.einsum('bhnjd,bhnje->bhnde', k_dec, xc)
        chunk_decay = jnp.exp(G[..., -1])

        def step(state, inp):
            dec, cs = inp
            return (state * dec + cs, state)
        init = jnp.zeros((B, H, D, D), hidden_states.dtype)
        _, prev = lax.scan(step, init, (chunk_decay.transpose(2, 0, 1)[..., None, None], cstates.transpose(2, 0, 1, 3, 4)))
        prev = prev.transpose(1, 2, 0, 3, 4)
        y_inter = jnp.einsum('bhnid,bhnde->bhnie', qc * jnp.exp(G)[..., None], prev)
        y = (y_intra + y_inter).reshape(B, H, L, D).transpose(0, 2, 1, 3)
        rms = jnp.sqrt(jnp.mean(jnp.square(y), axis=-1, keepdims=True) + RMS_EPS)
        y = y / rms * gnorm_w
        gate = (hidden_states @ Wg.T).reshape(B, L, H, D)
        y = y * (gate * jax.nn.sigmoid(gate))
        return y.reshape(B, L, H * D) @ Wo.T

    def _L0_ffn_ref(hidden_states, w_gate, w_up, w_down):
        import jax, jax.numpy as jnp
        import numpy as np
        EPS = 1e-05

        def _bitlinear(x, w):
            scale = jnp.mean(jnp.abs(w))
            q = jnp.round(jnp.clip(w / (scale + EPS), -1.0, 1.0))
            deq = q * scale
            return x @ deq.T
        gate = _bitlinear(hidden_states, w_gate)
        up = _bitlinear(hidden_states, w_up)
        inter = gate * up
        out = _bitlinear(inter, w_down)
        return out
    x = L0_attn_hidden_states
    x = x + 0.5 * _L0_ffn_ref(_layernorm(x, axis=-1), L0_ffn_w_gate, L0_ffn_w_up, L0_ffn_w_down)
    x = x + _L0_attn_ref(_layernorm(x, axis=-1), L0_attn_Wq, L0_attn_Wk, L0_attn_Wv, L0_attn_Wo, L0_attn_Wg, L0_attn_Win, L0_attn_dt_bias, L0_attn_A_log_bias, L0_attn_gnorm_w)
    x = x + 0.5 * _L0_ffn_ref(_layernorm(x, axis=-1), L0_ffn_w_gate, L0_ffn_w_up, L0_ffn_w_down)
    return x

_drawn_inputs = setup_inputs


def setup_inputs(seed=0):
    import zlib

    import numpy as np

    out = dict(_drawn_inputs(seed))
    spreads = {'L0_attn_dt_bias': (0.0, 2.0), 'L0_attn_gnorm_w': (1.0, 0.6)}
    factors = {}
    for name, (base, spread) in spreads.items():
        noise = np.random.default_rng([zlib.crc32(name.encode()), seed]).standard_normal(out[name].shape)
        drawn = base * np.exp(spread * noise) if base else spread * noise
        out[name] = jnp.asarray(drawn.astype(out[name].dtype))
    for name, factor in factors.items():
        out[name] = (out[name] * factor).astype(out[name].dtype)
    return out
```

```python
from contextlib import ExitStack

import concourse.bass as bass
from concourse import mybir
from concourse.bass import ds

P = 128
B, L, HID = 4, 256, 512
H, KVH, D = 32, 8, 128
REP = H // KVH
FF = 1376
TOK = B * L
NT = TOK // P
KT = HID // P
FT = -(-FF // P)
FP = FT * P
HALF = 512
NH2 = TOK // HALF
EPS = 1e-5
BIG = 1e30

ALU = mybir.AluOpType
ACT = mybir.ActivationFunctionType
F32, F32R, F16 = mybir.dt.float32, mybir.dt.float32r, mybir.dt.float16
AX = mybir.AxisListType.X

X_SCALE = 2048.0
INNER = 2.0 ** -3


class Signal:

    def __init__(self, ctx, nc, name, per=1, credit=False):
        self.sem, self.per, self.credit = ctx.enter_context(nc.semaphore(name)), per, credit

    def start(self, eng):
        if self.credit:
            eng.sem_inc(self.sem, self.per)

    def now(self, g, k):
        return (g + int(self.credit)) * self.per + k

    def last(self, g, k):
        assert self.credit and k >= 1
        return g * self.per + k


class Norm:

    def __init__(self, ctx, nc, tag, x, ident, hi, lo, scale):
        sb = lambda n, s, d=F32: ctx.enter_context(nc.sbuf_tensor(f"{n}_{tag}", s, d))
        self.x, self.ident, self.hi, self.lo, self.scale = x, ident, hi, lo, scale
        self.xn = sb("xn", [P, NT, HID])
        self.parts = sb("bn_parts", [P, NT, 6])
        self.mv = sb("mean_var", [P, NT, 2])
        self.var = sb("var_eps", [P, NT])
        self.rstd = sb("rstd", [P, NT])
        self.eps = sb("eps", [P, NT])
        self.power = sb("power", [P, NT])
        sem = lambda n: ctx.enter_context(nc.semaphore(f"{n}_{tag}"))
        self.consts, self.stat, self.aggr = sem("ln_consts"), sem("ln_stat"), sem("ln_aggr")
        self.veps, self.rstd_ready, self.xn_ready = sem("ln_veps"), sem("ln_rstd"), sem("ln_xn")
        self.t_ready, self.hi_done, self.lo_done = sem("ln_t"), sem("ln_hi"), sem("ln_lo")

    def pool(self, eng):
        eng.memset(self.eps[:, :], EPS).then_inc(self.consts, 1)
        eng.memset(self.power[:, :], -0.5).then_inc(self.consts, 1)
        eng.wait_ge(self.consts, 2)
        eng.wait_ge(self.aggr, NT)
        eng.tensor_tensor(self.var[:, :], self.mv[:, :, 1], self.eps[:, :], ALU.add).then_inc(self.veps, 1)
        eng.wait_ge(self.veps, 1)
        eng.tensor_tensor(self.rstd[:, :], self.var[:, :], self.power[:, :], ALU.pow).then_inc(self.rstd_ready, 1)

    def vector_stats(self, eng, t):
        eng.bn_stats(self.parts[:, t, :], self.x[:, t, :]).then_inc(self.stat, 1)
        eng.wait_ge(self.stat, t + 1)
        eng.bn_aggr(self.mv[:, t, :], self.parts[:, t, :]).then_inc(self.aggr, 1)

    def vector_norm(self, eng):
        eng.wait_ge(self.aggr, NT)
        eng.wait_ge(self.rstd_ready, 1)
        for t in range(NT):
            eng.tensor_scalar(self.xn[:, t, :], self.x[:, t, :], self.mv[:, t, 0:1], self.rstd[:, t:t + 1],
                              ALU.subtract, ALU.mult).then_inc(self.xn_ready, 1)

    def vector_lo(self, eng, banks):
        for t in range(NT):
            eng.wait_ge(self.hi_done, t + 1)
            hi = self.hi[:, :, t * P:(t + 1) * P]
            eng.scalar_tensor_tensor(out=self.lo[:, :, t * P:(t + 1) * P],
                                     in0=banks[t % 2][:, :].rearrange("p (k n) -> p k n", k=KT), scalar=self.scale,
                                     in1=hi.bitcast(F32) if hi.dtype == F32R else hi,
                                     op0=ALU.mult, op1=ALU.subtract).then_inc(self.lo_done, 1)

    def scalar_hi(self, eng, banks):
        for t in range(NT):
            eng.wait_ge(self.t_ready, t + 1)
            eng.activation(self.hi[:, :, t * P:(t + 1) * P], banks[t % 2][:, :].rearrange("p (k n) -> p k n", k=KT),
                           ACT.Copy, scale=self.scale).then_inc(self.hi_done, 1)

    def tensor(self, eng, banks):
        for t in range(NT):
            eng.wait_ge(self.xn_ready, t + 1)
            if t >= 2:
                eng.wait_ge(self.lo_done, t - 1)
            for k in range(KT):
                last = eng.transpose(banks[t % 2][:, k * P:(k + 1) * P], self.xn[:, t, k * P:(k + 1) * P],
                                     self.ident[:, :])
            last.then_inc(self.t_ready, 1)


def feed_forward(nc, tag, first, x, out_scale, ident, ones, const_in, x_in, weights, ternary, out):
    with ExitStack() as ctx:
        sb = lambda n, s, d=F32: ctx.enter_context(nc.sbuf_tensor(f"{n}_{tag}", s, d))
        sem = lambda n: ctx.enter_context(nc.semaphore(f"{n}_{tag}"))
        sig = lambda n, per: Signal(ctx, nc, f"{n}_{tag}", per, credit=True)
        bank = lambda n: ctx.enter_context(nc.psum_tensor(f"{n}_{tag}", [P, HALF], F32))

        x_hi, x_lo = sb("xT_hi", [P, KT, TOK], F16), sb("xT_lo", [P, KT, TOK], F16)
        q = [sb("q_gate", [P, KT, FP], F16), sb("q_up", [P, KT, FP], F16), sb("q_down", [P, FT, HID], F16)]
        q_gate, q_up, q_down = q
        inner_hi, inner_lo = sb("inner_hi", [P, FT, TOK], F16), sb("inner_lo", [P, FT, TOK], F16)
        gate, prod = sb("gate", [P, 2, HALF]), sb("prod", [P, 2, HALF])
        norm = Norm(ctx, nc, tag, x, ident, x_hi, x_lo, X_SCALE)
        t_bank = [bank("t0"), bank("t1")]
        gate_bank, up_bank = [bank("g0"), bank("g1")], [bank("u0"), bank("u1")]
        down_bank = [bank("d0"), bank("d1")]

        x_loaded, const_loaded = sem("x_loaded"), sem("const_loaded")
        w_loaded = [sem(f"w{m}_loaded") for m in range(3)]
        stored = sem("stored")
        gate_ready, up_ready = sig("gate_ready", 2), sig("up_ready", 2)
        gate_copied, prod_ready = sig("gate_copied", 2), sig("prod_ready", 2)
        inner_hi_done, inner_lo_done = sig("inner_hi_done", 2), sig("inner_lo_done", 2)
        down_ready, x_done = sig("down_ready", 2), sig("x_done", 2)

        flat = lambda a: a[:, :, :].rearrange("p a b -> p (a b)")
        NQ = 4
        CH = KT * FP // NQ
        N_W = FF * HID
        if first:
            raw = [sb(f"raw{m}", [P, KT * FP]) for m in range(3)]
            sums, total = sb("sums", [P, 3, NQ]), sb("total", [P, 3])
            above, below, mean = sb("above", [P, 3]), sb("below", [P, 3]), sb("mean", [P, 4])
            summed = [sem(f"summed{m}") for m in range(3)]
            sum_bcast, total_done, thresh = sem("sum_bcast"), sem("total_done"), sem("thresh")
            neg_done = [sem(f"neg{m}_done") for m in range(3)]
            q_done = [sem(f"q{m}_done") for m in range(3)]
            mean_done = sem("mean_done")
            sum_bank = [down_bank[0], down_bank[1], gate_bank[0]]
            ones_ready = sem("ones_ready")

        block = ctx.enter_context(nc.Block())

        @block.sync
        def _(sp):
            if first:
                sp.dma_start(ident[:, :], const_in).then_inc(const_loaded, 16)
                sp.dma_start(x[:, :, :], x_in).then_inc(x_loaded, 16)
                for m in range(3):
                    sp.dma_start(raw[m][:, :], weights[m]).then_inc(w_loaded[m], 16)
                for m in range(3):
                    sp.wait_ge(q_done[m], NQ)
                    sp.dma_start(ternary[m], flat(q[m])).then_inc(stored, 16)
                sp.wait_ge(stored, 48)
            else:
                for m in range(3):
                    sp.dma_start(flat(q[m]), ternary[m]).then_inc(w_loaded[m], 16)
                for t in range(NT):
                    sp.wait_ge(x_done.sem, x_done.now(t // 2, t % 2 + 1))
                    sp.dma_start(out[:, t, :], x[:, t, :]).then_inc(stored, 16)
                sp.wait_ge(stored, 16 * NT)

        @block.gpsimd
        def _(pool):
            norm.pool(pool)
            if first:
                for m in (1, 2):
                    pool.wait_ge(thresh, 2 * (m + 1))
                    for c in range(NQ):
                        pool.tensor_scalar(flat(q[m])[:, c * CH:(c + 1) * CH], raw[m][:, c * CH:(c + 1) * CH],
                                           below[:, m:m + 1], None, ALU.is_lt).then_inc(neg_done[m], 1)

        @block.scalar
        def _(act):
            gate_copied.start(act)
            inner_hi_done.start(act)
            if first:
                for m in range(3):
                    act.wait_ge(w_loaded[m], 16)
                    for c in range(NQ):
                        act.activation(flat(q[m])[:, c * CH:(c + 1) * CH], raw[m][:, c * CH:(c + 1) * CH], ACT.Abs,
                                       accum_out=sums[:, m, c:c + 1]).then_inc(summed[m], 1)
                    if m == 0:
                        norm.scalar_hi(act, t_bank)
            else:
                norm.scalar_hi(act, t_bank)

            with act.Fori(0, FT) as i:
                for s in range(2):
                    act.wait_ge(gate_ready.sem, gate_ready.now(i, s + 1))
                    act.wait_ge(prod_ready.sem, prod_ready.last(i, s + 1))
                    act.activation(gate[:, s, :], gate_bank[s][:, :], ACT.Copy,
                                   scale=INNER / X_SCALE ** 2).then_inc(gate_copied.sem, 1)
                for s in range(2):
                    act.wait_ge(prod_ready.sem, prod_ready.now(i, s + 1))
                    act.activation(inner_hi[:, ds(i, 1), s * HALF:(s + 1) * HALF].rearrange("p a n -> p (a n)"),
                                   prod[:, s, :], ACT.Copy).then_inc(inner_hi_done.sem, 1)

        @block.vector
        def _(dve):
            prod_ready.start(dve)
            inner_lo_done.start(dve)
            x_done.start(dve)
            if first:
                dve.memset(ones[:, :], 1.0).then_inc(ones_ready, 1)
                dve.wait_ge(x_loaded, 16)
            for t in range(NT):
                norm.vector_stats(dve, t)
            norm.vector_norm(dve)
            norm.vector_lo(dve, t_bank)
            if first:
                for m in range(3):
                    dve.wait_ge(sum_bcast, m + 1)
                    dve.reduce_sum(total[:, m:m + 1], sum_bank[m][:, 0:NQ], AX).then_inc(total_done, 1)
                    dve.wait_ge(total_done, m + 1)
                    dve.tensor_scalar(above[:, m:m + 1], total[:, m:m + 1], 0.5 / N_W, 0.5 * EPS,
                                      ALU.mult, ALU.add).then_inc(thresh, 1)
                    dve.tensor_scalar(below[:, m:m + 1], total[:, m:m + 1], -0.5 / N_W, -0.5 * EPS,
                                      ALU.mult, ALU.add).then_inc(thresh, 1)
                    dve.tensor_scalar(mean[:, m:m + 1], total[:, m:m + 1], 1.0 / N_W, None,
                                      ALU.mult).then_inc(mean_done, 1)
                    if m == 0:
                        dve.wait_ge(thresh, 2)
                        for c in range(NQ):
                            dve.tensor_scalar(flat(q[m])[:, c * CH:(c + 1) * CH], raw[m][:, c * CH:(c + 1) * CH],
                                              below[:, m:m + 1], None, ALU.is_lt).then_inc(neg_done[m], 1)
                    dve.wait_ge(thresh, 2 * (m + 1))
                    for c in range(NQ):
                        dve.wait_ge(neg_done[m], c + 1)
                        part = flat(q[m])[:, c * CH:(c + 1) * CH]
                        dve.scalar_tensor_tensor(out=part, in0=raw[m][:, c * CH:(c + 1) * CH],
                                                 scalar=above[:, m:m + 1], in1=part,
                                                 op0=ALU.is_gt, op1=ALU.subtract).then_inc(q_done[m], 1)
                dve.wait_ge(mean_done, 3)
                dve.tensor_scalar(mean[:, 3:4], mean[:, 0:1], mean[:, 1:2], mean[:, 2:3],
                                  ALU.mult, ALU.mult).then_inc(mean_done, 1)
                dve.wait_ge(mean_done, 4)
                dve.tensor_scalar(out_scale[:, :], mean[:, 3:4], 0.5 / INNER, None, ALU.mult).then_inc(mean_done, 1)
                dve.wait_ge(mean_done, 5)

            with dve.Fori(0, FT) as i:
                for s in range(2):
                    dve.wait_ge(gate_copied.sem, gate_copied.now(i, s + 1))
                    dve.wait_ge(up_ready.sem, up_ready.now(i, s + 1))
                    dve.wait_ge(inner_hi_done.sem, inner_hi_done.last(i, s + 1))
                    dve.wait_ge(inner_lo_done.sem, inner_lo_done.last(i, s + 1))
                    dve.tensor_tensor(prod[:, s, :], up_bank[s][:, :], gate[:, s, :],
                                      ALU.mult).then_inc(prod_ready.sem, 1)
                for s in range(2):
                    dve.wait_ge(inner_hi_done.sem, inner_hi_done.now(i, s + 1))
                    part = (slice(None), ds(i, 1), slice(s * HALF, (s + 1) * HALF))
                    dve.tensor_tensor(inner_lo[part].rearrange("p a n -> p (a n)"), prod[:, s, :],
                                      inner_hi[part].rearrange("p a n -> p (a n)"),
                                      ALU.subtract).then_inc(inner_lo_done.sem, 1)
            with dve.Fori(0, NT // 2) as i:
                for j in range(2):
                    dve.wait_ge(down_ready.sem, down_ready.now(i, j + 1))
                    xt = x[:, ds(2 * i + j, 1), :].rearrange("p a n -> p (a n)")
                    dve.scalar_tensor_tensor(out=xt, in0=down_bank[j][:, :], scalar=out_scale[:, 0:1], in1=xt,
                                             op0=ALU.mult, op1=ALU.add).then_inc(x_done.sem, 1)

        @block.tensor
        def _(pe):
            gate_ready.start(pe)
            up_ready.start(pe)
            down_ready.start(pe)
            if first:
                pe.wait_ge(const_loaded, 16)
                pe.wait_ge(ones_ready, 1)
            norm.tensor(pe, t_bank)
            if first:
                for m in range(3):
                    pe.wait_ge(summed[m], NQ)
                    pe.matmul(sum_bank[m][:, 0:NQ], ones[:, :], sums[:, m, :], start=True,
                              stop=True).then_inc(sum_bcast, 1)
                pe.wait_ge(total_done, 3)
                for m in range(2):
                    pe.wait_ge(q_done[m], NQ)
            else:
                for m in range(2):
                    pe.wait_ge(w_loaded[m], 16)
            pe.wait_ge(norm.lo_done, NT)

            with pe.Fori(0, FT) as i:
                for s in range(2):
                    cols = slice(s * HALF, (s + 1) * HALF)
                    for w, banks, ready, freed in ((q_gate, gate_bank, gate_ready, gate_copied),
                                                   (q_up, up_bank, up_ready, prod_ready)):
                        pe.wait_ge(freed.sem, freed.last(i, s + 1))
                        for k in range(KT):
                            for part, xs in enumerate((x_hi, x_lo)):
                                last = pe.matmul(banks[s][:, :], w[:, k, ds(i * P, P)], xs[:, k, cols],
                                                 start=k + part == 0, stop=k == KT - 1 and part == 1)
                        last.then_inc(ready.sem, 1)

            if first:
                pe.wait_ge(q_done[2], NQ)
            else:
                pe.wait_ge(w_loaded[2], 16)
            pe.wait_ge(inner_lo_done.sem, inner_lo_done.now(FT - 1, 2))
            pe.wait_ge(inner_hi_done.sem, inner_hi_done.now(FT - 1, 2))
            with pe.Fori(0, NT // 2) as i:
                for j in range(2):
                    pe.wait_ge(x_done.sem, x_done.last(i, j + 1))
                    for f in range(FT):
                        for part, inner in enumerate((inner_hi, inner_lo)):
                            last = pe.matmul(down_bank[j][:, :], inner[:, f, ds((2 * i + j) * P, P)], q_down[:, f, :],
                                             start=f + part == 0, stop=f == FT - 1 and part == 1)
                    last.then_inc(down_ready.sem, 1)


def attention_inputs(nc, x, ident, ones, x_hi, x_lo, stats, tri_in, w_v_in, w_in_in, dt_bias_in, a_log_in,
                     v_dram, g_dram):
    with ExitStack() as ctx:
        sb = lambda n, s, d=F32: ctx.enter_context(nc.sbuf_tensor(n, s, d))
        sem = lambda n: ctx.enter_context(nc.semaphore(n))
        bank = lambda n: ctx.enter_context(nc.psum_tensor(n, [P, HALF], F32))
        tri = sb("tri", [P, P])
        wv_raw, wv_hi, wv_lo = sb("wv_raw", [P, KT, KVH * D]), sb("wv_hi", [P, KT, KVH * D], F32R), \
            sb("wv_lo", [P, KT, KVH * D], F32R)
        win_raw, win_hi, win_lo = sb("win_raw", [P, KT, H]), sb("win_hi", [P, KT, P], F32R), \
            sb("win_lo", [P, KT, P], F32R)
        dt_bias, a_log = sb("dt_bias", [H, 1]), sb("a_log", [P, NT * H])
        v = sb("v_all", [P, NT, KVH * D])
        pre_t, g_t = sb("pre_t", [H, TOK]), sb("g_t", [H, TOK])
        wide = lambda n: sb(n, [P, NT * H])
        pre, mag, e, u, ln_u, d, rest, ru, corr, pos, a, g, G = map(
            wide, "pre mag expo one_plus ln_u back rest recip corr pos a_exp g cum".split())
        norm = Norm(ctx, nc, "attn", x, ident, x_hi, x_lo, 1.0)
        t_bank = [bank("at0"), bank("at1")]
        v_bank = [bank("v0"), bank("v1")]
        b = [bank(f"small{n}") for n in range(4)]

        loaded = {n: sem(f"{n}_loaded") for n in ("tri", "wv", "win", "bias", "alog")}
        cleared = sem("win_cleared")
        split_hi, split_lo = sem("split_hi"), sem("split_lo")
        pre_ready, pre_copied, nat_ready, step = sem("pre_ready"), sem("pre_copied"), sem("nat_ready"), sem("dt_step")
        act_step = sem("dt_act_step")
        cum_ready, cum_copied, gt_ready, gt_copied = sem("cum_ready"), sem("cum_copied"), sem("gt_ready"), \
            sem("gt_copied")
        v_ready, v_copied, stored = sem("v_ready"), sem("v_copied"), sem("vg_stored")
        dt_out = stats[:, 0:NT, :].rearrange("p t h -> p (t h)")
        block = ctx.enter_context(nc.Block())

        @block.sync
        def _(sp):
            sp.dma_start(tri[:, :], tri_in).then_inc(loaded["tri"], 16)
            sp.dma_start(win_raw[:, :, :], w_in_in).then_inc(loaded["win"], 16)
            sp.dma_start(wv_raw[:, :, :], w_v_in).then_inc(loaded["wv"], 16)
            sp.dma_start(dt_bias[:, :], dt_bias_in).then_inc(loaded["bias"], 16)
            sp.dma_start(a_log[:, :], a_log_in.partition_broadcast(P)).then_inc(loaded["alog"], 16)
            sp.wait_ge(gt_copied, 2)
            sp.dma_start(g_dram, g_t[:, :]).then_inc(stored, 16)
            for n in range(2 * NT):
                t, s = n // 2, n % 2
                sp.wait_ge(v_copied, n + 1)
                sp.dma_start(v_dram[4 * s:4 * s + 4, :, t, :].rearrange("g p e -> p g e"),
                             v[:, t, s * HALF:(s + 1) * HALF].rearrange("p (g e) -> p g e", g=4)).then_inc(stored, 16)
            sp.wait_ge(stored, 16 * (1 + 2 * NT))

        @block.gpsimd
        def _(pool):
            for m in (win_hi, win_lo):
                pool.memset(m[:, :, :].bitcast(F32), 0.0).then_inc(cleared, 1)
            norm.pool(pool)
            pool.wait_ge(split_hi, 1)
            pool.wait_ge(cleared, 2)
            pool.tensor_tensor(win_lo[:, :, 0:H], win_raw[:, :, :], win_hi[:, :, 0:H].bitcast(F32),
                               ALU.subtract).then_inc(split_lo, 1)
            for k in range(KT):
                pool.wait_ge(split_hi, k + 2)
                pool.tensor_tensor(wv_lo[:, k, :], wv_raw[:, k, :], wv_hi[:, k, :].bitcast(F32),
                                   ALU.subtract).then_inc(split_lo, 1)

        @block.scalar
        def _(act):
            act.wait_ge(loaded["win"], 16)
            act.wait_ge(cleared, 2)
            act.activation(win_hi[:, :, 0:H], win_raw[:, :, :], ACT.Copy).then_inc(split_hi, 1)
            act.wait_ge(loaded["wv"], 16)
            for k in range(KT):
                act.activation(wv_hi[:, k, :], wv_raw[:, k, :], ACT.Copy).then_inc(split_hi, 1)
            norm.scalar_hi(act, t_bank)
            act.wait_ge(loaded["bias"], 16)
            for s in range(2):
                act.wait_ge(pre_ready, s + 1)
                act.activation(pre_t[:, s * HALF:(s + 1) * HALF], b[s][0:H, :], ACT.Identity,
                               bias=dt_bias[:, 0:1]).then_inc(pre_copied, 1)

            def v_copy(n):
                t, s = n // 2, n % 2
                act.wait_ge(v_ready, n + 1)
                act.activation(v[:, t, s * HALF:(s + 1) * HALF], v_bank[n % 2][:, :], ACT.Copy).then_inc(v_copied, 1)

            act.wait_ge(step, 1)
            act.activation(mag[:, :], pre[:, :], ACT.Abs).then_inc(act_step, 1)
            act.wait_ge(act_step, 1)
            act.activation(e[:, :], mag[:, :], ACT.Exp, scale=-1.0).then_inc(act_step, 1)
            act.wait_ge(loaded["alog"], 16)
            act.activation(a[:, :], a_log[:, :], ACT.Exp).then_inc(act_step, 1)
            act.wait_ge(step, 2)
            act.activation(ln_u[:, :], u[:, :], ACT.Ln).then_inc(act_step, 1)
            v_copy(0)
            v_copy(1)
            act.wait_ge(cum_ready, 1)
            act.activation(G[:, :], b[0][:, 0:NT * H], ACT.Copy).then_inc(cum_copied, 1)
            v_copy(2)
            v_copy(3)
            for s in range(2):
                act.wait_ge(gt_ready, s + 1)
                act.activation(g_t[:, s * HALF:(s + 1) * HALF], b[2 + s][0:H, :], ACT.Copy).then_inc(gt_copied, 1)
            for n in range(4, 2 * NT):
                v_copy(n)

        @block.vector
        def _(dve):
            for t in range(NT):
                norm.vector_stats(dve, t)
            norm.vector_norm(dve)
            norm.vector_lo(dve, t_bank)
            done = [0]

            def own(ins):
                done[0] += 1
                ins.then_inc(step, 1)
                dve.wait_ge(step, done[0])

            dve.wait_ge(nat_ready, 1)
            own(dve.tensor_copy(pre[:, :], b[2][:, 0:NT * H]))
            dve.wait_ge(act_step, 2)
            own(dve.tensor_scalar(u[:, :], e[:, :], 1.0, None, ALU.add))
            own(dve.tensor_scalar(d[:, :], u[:, :], -1.0, None, ALU.add))
            own(dve.tensor_tensor(rest[:, :], e[:, :], d[:, :], ALU.subtract))
            own(dve.reciprocal(ru[:, :], u[:, :]))
            own(dve.tensor_tensor(corr[:, :], rest[:, :], ru[:, :], ALU.mult))
            own(dve.scalar_tensor_tensor(out=pos[:, :], in0=pre[:, :], scalar=0.0, in1=corr[:, :],
                                         op0=ALU.max, op1=ALU.add))
            dve.wait_ge(act_step, 4)
            own(dve.tensor_tensor(dt_out, pos[:, :], ln_u[:, :], ALU.add))
            own(dve.scalar_tensor_tensor(out=g[:, :], in0=dt_out, scalar=-1.0, in1=a[:, :],
                                         op0=ALU.mult, op1=ALU.mult))
            dve.wait_ge(cum_copied, 1)
            own(dve.tensor_scalar(stats[:, NT:2 * NT, :].rearrange("p t h -> p (t h)"), G[:, :], -1.0, None, ALU.mult))
            dve.wait_ge(cum_ready, 2)
            first_chunks = lambda m: m.rearrange("p (b c h) -> p b c h", b=B, c=2)[:, :, 0, :]
            own(dve.tensor_tensor(stats[:, 2 * NT:2 * NT + B, :], first_chunks(b[1][:, 0:NT * H]),
                                  first_chunks(G[:, :]), ALU.subtract))

        @block.tensor
        def _(pe):
            norm.tensor(pe, t_bank)
            pe.wait_ge(norm.lo_done, NT)
            pe.wait_ge(split_hi, 1)
            pe.wait_ge(split_lo, 1)
            for s in range(2):
                cols = slice(s * HALF, (s + 1) * HALF)
                for k in range(KT):
                    for n, (w, xs) in enumerate(((win_hi, x_hi), (win_hi, x_lo), (win_lo, x_hi))):
                        last = pe.matmul(b[s][:, :], w[:, k, :], xs[:, k, cols], start=k + n == 0,
                                         stop=k == KT - 1 and n == 2)
                last.then_inc(pre_ready, 1)
            pe.wait_ge(pre_copied, 2)
            for t in range(NT):
                last = pe.transpose(b[2][:, t * H:(t + 1) * H], pre_t[:, t * P:(t + 1) * P], ident[0:H, 0:H])
            last.then_inc(nat_ready, 1)

            def project_v(n):
                t, s = n // 2, n % 2
                if n >= 2:
                    pe.wait_ge(v_copied, n - 1)
                for k in range(KT):
                    for m, (xs, w) in enumerate(((x_hi, wv_hi), (x_lo, wv_hi), (x_hi, wv_lo))):
                        last = pe.matmul(v_bank[n % 2][:, :], xs[:, k, t * P:(t + 1) * P],
                                         w[:, k, s * HALF:(s + 1) * HALF], start=k + m == 0,
                                         stop=k == KT - 1 and m == 2)
                last.then_inc(v_ready, 1)

            pe.wait_ge(split_hi, 1 + KT)
            pe.wait_ge(split_lo, 1 + KT)
            project_v(0)
            project_v(1)
            pe.wait_ge(loaded["tri"], 16)
            pe.wait_ge(step, 9)
            pe.matmul(b[0][:, 0:NT * H], tri[:, :], g[:, :], start=True, stop=True).then_inc(cum_ready, 1)
            pe.matmul(b[1][:, 0:NT * H], ones[:, :], g[:, :], start=True, stop=True).then_inc(cum_ready, 1)
            project_v(2)
            pe.wait_ge(cum_copied, 1)
            for s in range(2):
                for t in range(4):
                    tt = 4 * s + t
                    last = pe.transpose(b[2 + s][0:H, t * P:(t + 1) * P], G[:, tt * H:(tt + 1) * H], ident[:, :])
                last.then_inc(gt_ready, 1)
            for n in range(3, 2 * NT):
                project_v(n)


PLAN = [("K", 0), ("K", 1)] + [("Q", n) for n in range(7)] + [("E", 0), ("Q", 7)] + [
    (s[0], int(s[1])) for s in (
        "S0 E1 G0 G1 Y0 G2 S1 Y1 G3 E2 T0 Y2 G4 S2 T1 Y3 G5 E3 T2 O0 Y4 G6 S3 T3 O1 Y5 G7 T4 O2 Y6 O3 T5 Y7 "
        "O4 T6 O5 T7 O6 O7").split()]
NR = 2 + 2 * REP
SHARED = [p for p in PLAN if p[0] in "GO"]
BLOCKS = ((0, 0), (0, 1), (1, 1))


def attention(nc, x, ident, x_hi, x_lo, stats, w_q_in, w_k_in, w_g_in, w_o_in, table_in, gnorm_in, v_dram, g_dram):
    with ExitStack() as ctx:
        sb = lambda n, s, d=F32: ctx.enter_context(nc.sbuf_tensor(n, s, d))
        sem = lambda n: ctx.enter_context(nc.semaphore(n))
        sig = lambda n, per: Signal(ctx, nc, n, per, credit=True)
        bank = lambda n: ctx.enter_context(nc.psum_tensor(n, [P, HALF], F32))

        cos, sin, mask = sb("cos", [P, HALF]), sb("sin_signed", [P, HALF]), sb("causal_mask", [P, HALF])
        gnorm, eps4, power = sb("gnorm", [P, 1]), sb("eps4", [P, REP]), sb("neg_half", [P, REP])
        raw_k, raw_g = sb("raw_k", [P, KT, D]), sb("raw_g", [P, KT, HALF])
        raw_qo = sb("raw_qo", [P, KT, HALF])
        w = {n: (sb(f"w{n}_hi", [P, KT, D if n == "k" else HALF], F32R),
                 sb(f"w{n}_lo", [P, KT, D if n == "k" else HALF], F32R)) for n in "kqgo"}
        raw = {"k": raw_k, "q": raw_qo, "g": raw_g, "o": raw_qo}
        k_t, q_t = sb("k_t", [P, TOK]), sb("q_t", [P, REP, TOK])
        v = sb("v", [P, NT, D])
        g_rows = sb("g_rows", [P, 2, REP, L])
        g_masked = sb("g_masked", [P, REP, P])
        prob = sb("prob", [P, 2, len(BLOCKS), REP, P])
        rot_a, rot_b = sb("rot_cos", [P, 2, HALF]), sb("rot_sin", [P, 2, HALF])
        z = sb("z", [P, 4, REP, D])
        z_hi, z_lo = sb("z_t_hi", [P, 2, REP, P], F32R), sb("z_t_lo", [P, 2, REP, P], F32R)
        junk = sb("squares", [P, REP, D], F16)
        sumsq, sum_eps, rinv = sb("sumsq", [P, NT, REP]), sb("sum_eps", [P, NT, REP]), sb("rinv", [P, NT, REP])
        head = sb("head_stats", [P, 2 * NT + B, REP])
        rot_bank, mul_bank, s_bank = [bank("r0"), bank("r1")], [bank("j0"), bank("j1")], [bank("s0"), bank("s1")]
        y_bank, z_bank = bank("y"), bank("zt")

        table_loaded, consts_ready = sem("table_loaded"), sem("attn_consts")
        ld_k, ld_g, ld_v = (Signal(ctx, nc, f"load_{n}", 16) for n in "kgv")
        ld_qo = Signal(ctx, nc, "load_qo", 32)
        ld_rows = [Signal(ctx, nc, f"load_rows{n}", 32) for n in range(2)]
        hi_done, lo_done = sig("w_hi_done", 4), sig("w_lo_done", 4)
        rot_ready, cos_done, swap_done = sig("rot_ready", NR), sig("cos_done", NR), sig("swap_done", NR)
        sin_done, rot_done = sig("sin_done", NR), sig("rot_done", NR)
        mul_ready = sig("mul_ready", len(SHARED))
        tanh_done, silu_done, x_added = sig("tanh_done", NT), sig("silu_done", NT), sig("x_added", NT)
        mask_done, decay_done = sig("mask_done", 2 * B), sig("decay_done", 3 * B)
        score_ready, prob_done = sig("score_ready", 3 * B), sig("prob_done", 3 * B)
        y_ready, square_done, eps_done, rinv_done = (sig(n, NT) for n in ("y_ready", "square_done", "eps_done",
                                                                         "rinv_done"))
        z_done, zt_ready, zhi_done, zlo_done = (sig(n, NT) for n in ("z_done", "zt_ready", "zhi_done", "zlo_done"))
        head_copied = sig("head_copied", 1)

        def used(sg, g, n, ring):
            return sg.now(g, n - ring + 1) if n >= ring else sg.last(g, sg.per + n - ring + 1)

        def mul_at(what, t):
            return SHARED.index((what, t))

        block = ctx.enter_context(nc.Block())

        @block.sync
        def _(sp):
            for n, m in enumerate((cos, sin, mask)):
                sp.dma_start(m[:, :], table_in[:, n, :]).then_inc(table_loaded, 16)
            sp.dma_start(gnorm[:, :], gnorm_in).then_inc(table_loaded, 16)
            with sp.Fori(0, KVH) as g:
                pick = lambda a: a[ds(g, 1), :, :, :].rearrange("a p k n -> (a p) k n")
                sp.wait_ge(lo_done.sem, lo_done.last(g, 1))
                sp.dma_start(raw_k[:, :, :], pick(w_k_in)).then_inc(ld_k.sem, 16)
                sp.wait_ge(lo_done.sem, lo_done.last(g, 4))
                sp.dma_start(raw_qo[:, :, :], pick(w_q_in)).then_inc(ld_qo.sem, 16)
                sp.dma_start(raw_g[:, :, :], pick(w_g_in)).then_inc(ld_g.sem, 16)
                sp.wait_ge(lo_done.sem, lo_done.now(g, 2))
                sp.dma_start(raw_qo[:, :, :], pick(w_o_in)).then_inc(ld_qo.sem, 16)
                sp.wait_ge(y_ready.sem, y_ready.last(g, NT))
                sp.dma_start(v[:, :, :], pick(v_dram)).then_inc(ld_v.sem, 16)
                for b in range(B):
                    sp.wait_ge(decay_done.sem, decay_done.now(g, 3 * (b - 1)) if b >= 2 else
                               decay_done.last(g, 3 * (B + b - 1)))
                    sp.dma_start(g_rows[:, b % 2, :, :],
                                 g_dram[ds(g * REP, REP), b * L:(b + 1) * L].partition_broadcast(P)
                                 ).then_inc(ld_rows[b % 2].sem, 16)

        @block.gpsimd
        def _(pool):
            for sg in (lo_done, sin_done, mask_done, eps_done, rinv_done):
                sg.start(pool)
            pool.memset(eps4[:, :], 4 * EPS).then_inc(consts_ready, 1)
            pool.memset(power[:, :], -0.5).then_inc(consts_ready, 1)
            pool.wait_ge(consts_ready, 2)
            pool.wait_ge(table_loaded, 64)
            with pool.Fori(0, KVH) as g:

                def split_lo(n):
                    name = "kqgo"[n]
                    pool.wait_ge(hi_done.sem, hi_done.now(g, n + 1))
                    pool.tensor_tensor(w[name][1][:, :, :], raw[name][:, :, :], w[name][0][:, :, :].bitcast(F32),
                                       ALU.subtract).then_inc(lo_done.sem, 1)

                split_lo(0)
                split_lo(1)
                for what, n in PLAN:
                    if what in "KQ":
                        r = n if what == "K" else 2 + n
                        pool.wait_ge(swap_done.sem, swap_done.now(g, r + 1))
                        pool.tensor_tensor(rot_b[:, r % 2, :], rot_b[:, r % 2, :], sin[:, :],
                                           ALU.mult).then_inc(sin_done.sem, 1)
                        if r == 3:
                            split_lo(2)
                        if r == 6:
                            split_lo(3)
                    elif what == "E":
                        rows = g_rows[:, n % 2, :, :]
                        causal = mask[:, :].rearrange("p (h i) -> p h i", h=REP)
                        pool.wait_ge(ld_rows[n % 2].sem, ld_rows[n % 2].now(g, 16 * (n // 2 + 1)))
                        if n >= 1:
                            pool.wait_ge(decay_done.sem, decay_done.now(g, 3 * n))
                        else:
                            pool.wait_ge(decay_done.sem, decay_done.last(g, 3 * B))
                        pool.tensor_tensor(g_masked[:, :, :], rows[:, :, P:L], causal, ALU.add).then_inc(mask_done.sem, 1)
                        pool.tensor_tensor(rows[:, :, 0:P], rows[:, :, 0:P], causal, ALU.add).then_inc(mask_done.sem, 1)
                    elif what == "Y":
                        pool.wait_ge(square_done.sem, square_done.now(g, n + 1))
                        pool.tensor_tensor(sum_eps[:, n, :], sumsq[:, n, :], eps4[:, :], ALU.add).then_inc(eps_done.sem, 1)
                        pool.wait_ge(eps_done.sem, eps_done.now(g, n + 1))
                        pool.tensor_tensor(rinv[:, n, :], sum_eps[:, n, :], power[:, :], ALU.pow).then_inc(rinv_done.sem, 1)

        @block.scalar
        def _(act):
            for sg in (hi_done, swap_done, tanh_done, decay_done, square_done, zhi_done):
                sg.start(act)
            act.wait_ge(table_loaded, 64)
            with act.Fori(0, KVH) as g:

                def split_hi(n):
                    name = "kqgo"[n]
                    loaded, count = ((ld_k, 16), (ld_qo, 16), (ld_g, 16), (ld_qo, 32))[n]
                    act.wait_ge(loaded.sem, loaded.now(g, count))
                    user, k = ((rot_ready, 2), (rot_ready, NR), (mul_ready, mul_at("G", NT - 1) + 1),
                               (mul_ready, len(SHARED)))[n]
                    act.wait_ge(user.sem, user.last(g, k))
                    act.activation(w[name][0][:, :, :], raw[name][:, :, :], ACT.Copy).then_inc(hi_done.sem, 1)

                split_hi(0)
                split_hi(1)
                for what, n in PLAN:
                    if what in "KQ":
                        r = n if what == "K" else 2 + n
                        act.wait_ge(rot_ready.sem, rot_ready.now(g, r + 1))
                        act.wait_ge(rot_done.sem, used(rot_done, g, r, 2))
                        act.activation(rot_b[0:64, r % 2, :], rot_bank[r % 2][64:128, :], ACT.Copy)
                        act.activation(rot_b[64:128, r % 2, :], rot_bank[r % 2][0:64, :],
                                       ACT.Copy).then_inc(swap_done.sem, 1)
                        if r == 3:
                            split_hi(2)
                        if r == 6:
                            split_hi(3)
                    elif what == "E":
                        act.wait_ge(head_copied.sem, head_copied.now(g, 1))
                        act.wait_ge(y_ready.sem, used(y_ready, g, 2 * n + 1, 4))
                        act.wait_ge(mask_done.sem, mask_done.now(g, 2 * n + 2))
                        for m, (kc, qc) in enumerate(BLOCKS):
                            for h in range(REP):
                                if m == 0:
                                    rows, bias = g_rows[:, n % 2, h, 0:P], head[:, NT + 2 * n, h:h + 1]
                                elif m == 1:
                                    rows, bias = g_rows[:, n % 2, h, P:L], head[:, 2 * NT + n, h:h + 1]
                                else:
                                    rows, bias = g_masked[:, h, :], head[:, NT + 2 * n + 1, h:h + 1]
                                last = act.activation(prob[:, n % 2, m, h, :], rows, ACT.Exp, bias=bias)
                            last.then_inc(decay_done.sem, 1)
                    elif what == "G":
                        m = mul_at("G", n)
                        act.wait_ge(mul_ready.sem, mul_ready.now(g, m + 1))
                        act.wait_ge(zt_ready.sem, used(zt_ready, g, n, 4))
                        act.activation(z[:, n % 4, :, :].rearrange("p h e -> p (h e)"), mul_bank[m % 2][:, :], ACT.Tanh,
                                       scale=0.5).then_inc(tanh_done.sem, 1)
                    elif what == "Y":
                        act.wait_ge(y_ready.sem, y_ready.now(g, n + 1))
                        act.wait_ge(square_done.sem, used(square_done, g, n, 1))
                        for h in range(REP):
                            last = act.activation(junk[:, h, :], y_bank[:, h * D:(h + 1) * D], ACT.Square,
                                                  scale=(4.0 / D) ** 0.5, accum_out=sumsq[:, n, h:h + 1])
                        last.then_inc(square_done.sem, 1)
                    elif what == "T":
                        act.wait_ge(zt_ready.sem, zt_ready.now(g, n + 1))
                        o = mul_at("O", (n - 2) % NT) + 1
                        act.wait_ge(mul_ready.sem, mul_ready.now(g, o) if n >= 2 else mul_ready.last(g, o))
                        act.activation(z_hi[:, n % 2, :, :].rearrange("p h i -> p (h i)"), z_bank[:, :], ACT.Copy,
                                       scale=gnorm[:, 0:1]).then_inc(zhi_done.sem, 1)

        @block.vector
        def _(dve):
            for sg in (cos_done, rot_done, silu_done, prob_done, z_done, zlo_done, x_added, head_copied):
                sg.start(dve)
            dve.wait_ge(table_loaded, 64)
            with dve.Fori(0, KVH) as g:
                dve.wait_ge(decay_done.sem, decay_done.last(g, 3 * B))
                dve.wait_ge(prob_done.sem, prob_done.last(g, 3 * B))
                dve.tensor_copy(head[:, :, :], stats[:, :, ds(g * REP, REP)]).then_inc(head_copied.sem, 1)
                dve.wait_ge(score_ready.sem, score_ready.last(g, 3 * B))

                def rotate(r):
                    dve.wait_ge(sin_done.sem, sin_done.now(g, r + 1))
                    dve.wait_ge(cos_done.sem, cos_done.now(g, r + 1))
                    if r < 2:
                        dst = k_t[:, r * HALF:(r + 1) * HALF]
                    else:
                        s, h = (r - 2) // REP, (r - 2) % REP
                        dst = q_t[:, h, s * HALF:(s + 1) * HALF]
                    dve.tensor_tensor(dst, rot_a[:, r % 2, :], rot_b[:, r % 2, :], ALU.add).then_inc(rot_done.sem, 1)

                for what, n in PLAN:
                    if what in "KQ":
                        r = n if what == "K" else 2 + n
                        dve.wait_ge(swap_done.sem, swap_done.now(g, r + 1))
                        dve.wait_ge(rot_done.sem, used(rot_done, g, r, 2))
                        dve.tensor_tensor(rot_a[:, r % 2, :], rot_bank[r % 2][:, :], cos[:, :],
                                          ALU.mult).then_inc(cos_done.sem, 1)
                        if r >= 1:
                            rotate(r - 1)
                        if r == NR - 1:
                            rotate(r)
                    elif what == "S":
                        dve.wait_ge(head_copied.sem, head_copied.now(g, 1))
                        for m, (kc, qc) in enumerate(BLOCKS):
                            i = 3 * n + m
                            dve.wait_ge(score_ready.sem, score_ready.now(g, i + 1))
                            dve.wait_ge(decay_done.sem, decay_done.now(g, i + 1))
                            for h in range(REP):
                                p = prob[:, n % 2, m, h, :]
                                last = dve.scalar_tensor_tensor(out=p, in0=s_bank[i % 2][:, h * P:(h + 1) * P],
                                                                scalar=head[:, 2 * n + kc, h:h + 1], in1=p,
                                                                op0=ALU.mult, op1=ALU.mult)
                            last.then_inc(prob_done.sem, 1)
                    elif what == "G":
                        m = mul_at("G", n)
                        zt = z[:, n % 4, :, :].rearrange("p h e -> p (h e)")
                        dve.wait_ge(tanh_done.sem, tanh_done.now(g, n + 1))
                        dve.scalar_tensor_tensor(out=zt, in0=zt, scalar=1.0, in1=mul_bank[m % 2][:, :],
                                                 op0=ALU.add, op1=ALU.mult).then_inc(silu_done.sem, 1)
                    elif what == "Y":
                        dve.wait_ge(rinv_done.sem, rinv_done.now(g, n + 1))
                        dve.wait_ge(silu_done.sem, silu_done.now(g, n + 1))
                        for h in range(REP):
                            zt = z[:, n % 4, h, :]
                            last = dve.scalar_tensor_tensor(out=zt, in0=y_bank[:, h * D:(h + 1) * D],
                                                            scalar=rinv[:, n, h:h + 1], in1=zt,
                                                            op0=ALU.mult, op1=ALU.mult)
                        last.then_inc(z_done.sem, 1)
                    elif what == "T":
                        dve.wait_ge(zhi_done.sem, zhi_done.now(g, n + 1))
                        dve.scalar_tensor_tensor(out=z_lo[:, n % 2, :, :].rearrange("p h i -> p (h i)"),
                                                 in0=z_bank[:, :], scalar=gnorm[:, 0:1],
                                                 in1=z_hi[:, n % 2, :, :].rearrange("p h i -> p (h i)").bitcast(F32),
                                                 op0=ALU.mult, op1=ALU.subtract).then_inc(zlo_done.sem, 1)
                    elif what == "O":
                        m = mul_at("O", n)
                        dve.wait_ge(mul_ready.sem, mul_ready.now(g, m + 1))
                        dve.wait_ge(x_added.sem, x_added.last(g, n + 1))
                        dve.tensor_tensor(x[:, n, :], mul_bank[m % 2][:, :], x[:, n, :], ALU.add).then_inc(x_added.sem, 1)

        @block.tensor
        def _(pe):
            for sg in (rot_ready, mul_ready, score_ready, y_ready, zt_ready):
                sg.start(pe)

            def three_pass(out, a, b, k_range):
                for k in k_range:
                    for n, (i, j) in enumerate(((0, 0), (0, 1), (1, 0))):
                        last = pe.matmul(out, a(k)[i], b(k)[j], start=k == k_range[0] and n == 0,
                                         stop=k == k_range[-1] and n == 2)
                return last

            with pe.Fori(0, KVH) as g:

                def split_ready(n):
                    pe.wait_ge(hi_done.sem, hi_done.now(g, n + 1))
                    pe.wait_ge(lo_done.sem, lo_done.now(g, n + 1))

                def mul_free(m):
                    what, t = SHARED[(m - 2) % len(SHARED)]
                    sg = silu_done if what == "G" else x_added
                    pe.wait_ge(sg.sem, sg.now(g, t + 1) if m >= 2 else sg.last(g, t + 1))

                for what, n in PLAN:
                    if what in "KQ":
                        if n == 0:
                            split_ready("KQ".index(what))
                        r = n if what == "K" else 2 + n
                        pe.wait_ge(cos_done.sem, used(cos_done, g, r, 2))
                        s, h = (n, 0) if what == "K" else (n // REP, n % REP)
                        wt, cols = w[what.lower()], slice(s * HALF, (s + 1) * HALF)
                        three_pass(rot_bank[r % 2][:, :],
                                   lambda k: [m[:, k, h * D:(h + 1) * D] for m in wt],
                                   lambda k: (x_hi[:, k, cols], x_lo[:, k, cols]),
                                   range(KT)).then_inc(rot_ready.sem, 1)
                    elif what == "G":
                        if n == 0:
                            split_ready(2)
                        m = mul_at("G", n)
                        mul_free(m)
                        rows = slice(n * P, (n + 1) * P)
                        three_pass(mul_bank[m % 2][:, :], lambda k: (x_hi[:, k, rows], x_lo[:, k, rows]),
                                   lambda k: [a[:, k, :] for a in w["g"]], range(KT)).then_inc(mul_ready.sem, 1)
                    elif what == "S":
                        pe.wait_ge(rot_done.sem, rot_done.now(g, 2 + REP * (n // 2 + 1)))
                        for m, (kc, qc) in enumerate(BLOCKS):
                            i = 3 * n + m
                            pe.wait_ge(prob_done.sem, used(prob_done, g, i, 2))
                            kt, qt = 2 * n + kc, 2 * n + qc
                            pe.matmul(s_bank[i % 2][:, :], k_t[:, kt * P:(kt + 1) * P],
                                      q_t[:, :, qt * P:(qt + 1) * P], start=True,
                                      stop=True).then_inc(score_ready.sem, 1)
                    elif what == "Y":
                        b, qc = n // 2, n % 2
                        if n == 0:
                            pe.wait_ge(ld_v.sem, ld_v.now(g, 16))
                        pe.wait_ge(prob_done.sem, prob_done.now(g, 3 * b + (3 if qc else 1)))
                        pe.wait_ge(z_done.sem, used(z_done, g, n, 1))
                        mine = [(m, kc) for m, (kc, c) in enumerate(BLOCKS) if c == qc]
                        for h in range(REP):
                            for m, kc in mine:
                                last = pe.matmul(y_bank[:, h * D:(h + 1) * D], prob[:, b % 2, m, h, :],
                                                 v[:, 2 * b + kc, :], start=m == mine[0][0], stop=m == mine[-1][0])
                        last.then_inc(y_ready.sem, 1)
                    elif what == "T":
                        pe.wait_ge(z_done.sem, z_done.now(g, n + 1))
                        pe.wait_ge(zlo_done.sem, used(zlo_done, g, n, 1))
                        for h in range(REP):
                            last = pe.transpose(z_bank[:, h * P:(h + 1) * P], z[:, n % 4, h, :], ident[:, :])
                        last.then_inc(zt_ready.sem, 1)
                    elif what == "O":
                        if n == 0:
                            split_ready(3)
                        m = mul_at("O", n)
                        mul_free(m)
                        pe.wait_ge(zhi_done.sem, zhi_done.now(g, n + 1))
                        pe.wait_ge(zlo_done.sem, zlo_done.now(g, n + 1))
                        three_pass(mul_bank[m % 2][:, :], lambda h: (z_hi[:, n % 2, h, :], z_lo[:, n % 2, h, :]),
                                   lambda h: [a[:, h, :] for a in w["o"]], range(REP)).then_inc(mul_ready.sem, 1)


def build(nc, args, out):
    (x_in, w_q, w_k, w_v, w_g, w_o, w_in, dt_bias, a_log, gnorm, w_gate, w_up, w_down, squares, tables) = args
    with ExitStack() as ctx:
        sb = lambda n, s, d=F32: ctx.enter_context(nc.sbuf_tensor(n, s, d))
        x = sb("x", [P, NT, HID])
        ident, ones, out_scale = sb("ident", [P, P]), sb("ones", [P, P]), sb("out_scale", [P, 1])
        ternary = [nc.dram_tensor(f"ternary{m}", [P, KT * FP], F16, kind="Internal").ap() for m in range(3)]
        v_dram = nc.dram_tensor("v_by_head", [KVH, P, NT, D], F32, kind="Internal").ap()
        g_dram = nc.dram_tensor("g_rows_dram", [H, TOK], F32, kind="Internal").ap()
        tiles = lambda a: a.rearrange("(t p) n -> p t n", p=P)
        feed_forward(nc, "ffn1", True, x, out_scale, ident, ones, squares[:, 0, :], tiles(x_in),
                     (w_gate, w_up, w_down), ternary, None)
        with ExitStack() as inner:
            sbi = lambda n, s, d=F32: inner.enter_context(nc.sbuf_tensor(n, s, d))
            x_hi, x_lo = sbi("ax_hi", [P, KT, TOK], F32R), sbi("ax_lo", [P, KT, TOK], F32R)
            stats = sbi("stats", [P, 2 * NT + B, H])
            attention_inputs(nc, x, ident, ones, x_hi, x_lo, stats, squares[:, 1, :], w_v, w_in, dt_bias, a_log,
                             v_dram, g_dram)
            attention(nc, x, ident, x_hi, x_lo, stats, w_q, w_k, w_g, w_o, tables, gnorm, v_dram, g_dram)
        feed_forward(nc, "ffn2", False, x, out_scale, ident, ones, None, None, None, ternary, tiles(out))


def kernel(L0_attn_hidden_states, L0_attn_Wq, L0_attn_Wk, L0_attn_Wv, L0_attn_Wo, L0_attn_Wg, L0_attn_Win,
           L0_attn_dt_bias, L0_attn_A_log_bias, L0_attn_gnorm_w, L0_ffn_w_gate, L0_ffn_w_up, L0_ffn_w_down):
    import numpy as np
    import concourse.bacc as bacc
    from concourse.bass_utils import run_bass_kernel_spmd

    a = np.asarray
    by_head = lambda w: a(w).reshape(KVH, -1, KT, P).transpose(0, 3, 2, 1)
    contracted = lambda w: a(w).reshape(-1, KT, P).transpose(2, 1, 0)
    padded = np.zeros((FP - FF, HID), np.float32)
    inner_first = lambda w: np.concatenate([a(w), padded])
    gate, up = (contracted(inner_first(w)).reshape(P, KT * FP) for w in (L0_ffn_w_gate, L0_ffn_w_up))
    down = inner_first(a(L0_ffn_w_down).T).reshape(FT, P, HID).transpose(1, 0, 2).reshape(P, FT * HID)
    w_o = a(L0_attn_Wo).reshape(HID, KVH, REP, D).transpose(1, 3, 2, 0)

    i = np.arange(P)
    squares = np.stack([np.eye(P), i[:, None] <= i[None, :]], 1).astype(np.float32)
    inv_freq = (np.float32(1) / np.power(np.float32(10000), np.arange(0, D, 2, dtype=np.float32) / np.float32(D)))
    ang = (np.arange(L, dtype=np.float32)[:, None] * inv_freq.astype(np.float32)).astype(np.float64)
    cos = np.tile(np.concatenate([np.cos(ang), np.cos(ang)], 1).T, (1, HALF // L))
    sin = np.tile(np.concatenate([-np.sin(ang), np.sin(ang)], 1).T, (1, HALF // L))
    mask = np.tile(np.where(i[:, None] <= i[None, :], 0.0, -BIG), (1, REP))
    tables = np.stack([cos, sin, mask], 1).astype(np.float32)

    ins = {
        "x_in": a(L0_attn_hidden_states).reshape(TOK, HID),
        "w_q": by_head(L0_attn_Wq), "w_k": by_head(L0_attn_Wk), "w_v": contracted(L0_attn_Wv),
        "w_g": by_head(L0_attn_Wg), "w_o": w_o, "w_in": contracted(L0_attn_Win),
        "dt_bias": a(L0_attn_dt_bias).reshape(H, 1), "a_log": np.tile(a(L0_attn_A_log_bias), NT),
        "gnorm": a(L0_attn_gnorm_w).reshape(D, 1), "w_gate": gate, "w_up": up, "w_down": down,
        "squares": squares, "tables": tables,
    }
    nc = bacc.Bacc("TRN2", target_bir_lowering=False, num_devices=1)
    arrays, args = {}, []
    for name, v in ins.items():
        arrays[f"in_{name}"] = np.ascontiguousarray(v)
        args.append(nc.dram_tensor(f"in_{name}", arrays[f"in_{name}"].shape, mybir.dt.from_np(arrays[f"in_{name}"].dtype),
                                   kind="ExternalInput").ap())
    out = nc.dram_tensor("out", (TOK, HID), F32, kind="ExternalOutput").ap()
    build(nc, args, out)
    r = run_bass_kernel_spmd(nc, [arrays], core_ids=[0])
    return r.results[0]["out"].reshape(B, L, HID)
```

```python
from contextlib import ExitStack

import concourse.bass as bass
from concourse import mybir
from concourse.bass import ds

P = 128
B, L, HID = 4, 256, 512
H, KVH, D = 32, 8, 128
REP = H // KVH
FF = 1376
TOK = B * L
NT = TOK // P
KT = HID // P
FT = -(-FF // P)
FP = FT * P
HALF = 512
NH2 = TOK // HALF
EPS = 1e-5
BIG = 1e30

ALU = mybir.AluOpType
ACT = mybir.ActivationFunctionType
F32, F32R, F16 = mybir.dt.float32, mybir.dt.float32r, mybir.dt.float16
AX = mybir.AxisListType.X

X_SCALE = 2048.0
INNER = 2.0 ** -3


class Signal:

    def __init__(self, ctx, nc, name, per=1, credit=False):
        self.sem, self.per, self.credit = ctx.enter_context(nc.semaphore(name)), per, credit

    def start(self, eng):
        if self.credit:
            eng.sem_inc(self.sem, self.per)

    def now(self, g, k):
        return (g + int(self.credit)) * self.per + k

    def last(self, g, k):
        assert self.credit and k >= 1
        return g * self.per + k


class Norm:

    def __init__(self, ctx, nc, tag, x, ident, hi, lo, scale):
        sb = lambda n, s, d=F32: ctx.enter_context(nc.sbuf_tensor(f"{n}_{tag}", s, d))
        self.x, self.ident, self.hi, self.lo, self.scale = x, ident, hi, lo, scale
        self.xn = sb("xn", [P, NT, HID])
        self.parts = sb("bn_parts", [P, NT, 6])
        self.mv = sb("mean_var", [P, NT, 2])
        self.var = sb("var_eps", [P, NT])
        self.rstd = sb("rstd", [P, NT])
        self.eps = sb("eps", [P, NT])
        self.power = sb("power", [P, NT])
        sem = lambda n: ctx.enter_context(nc.semaphore(f"{n}_{tag}"))
        self.consts, self.stat, self.aggr = sem("ln_consts"), sem("ln_stat"), sem("ln_aggr")
        self.veps, self.rstd_ready, self.xn_ready = sem("ln_veps"), sem("ln_rstd"), sem("ln_xn")
        self.t_ready, self.hi_done, self.lo_done = sem("ln_t"), sem("ln_hi"), sem("ln_lo")

    def pool(self, eng):
        eng.memset(self.eps[:, :], EPS).then_inc(self.consts, 1)
        eng.memset(self.power[:, :], -0.5).then_inc(self.consts, 1)
        eng.wait_ge(self.consts, 2)
        eng.wait_ge(self.aggr, NT)
        eng.tensor_tensor(self.var[:, :], self.mv[:, :, 1], self.eps[:, :], ALU.add).then_inc(self.veps, 1)
        eng.wait_ge(self.veps, 1)
        eng.tensor_tensor(self.rstd[:, :], self.var[:, :], self.power[:, :], ALU.pow).then_inc(self.rstd_ready, 1)

    def vector_stats(self, eng, t):
        eng.bn_stats(self.parts[:, t, :], self.x[:, t, :]).then_inc(self.stat, 1)
        eng.wait_ge(self.stat, t + 1)
        eng.bn_aggr(self.mv[:, t, :], self.parts[:, t, :]).then_inc(self.aggr, 1)

    def vector_norm(self, eng):
        eng.wait_ge(self.aggr, NT)
        eng.wait_ge(self.rstd_ready, 1)
        for t in range(NT):
            eng.tensor_scalar(self.xn[:, t, :], self.x[:, t, :], self.mv[:, t, 0:1], self.rstd[:, t:t + 1],
                              ALU.subtract, ALU.mult).then_inc(self.xn_ready, 1)

    def vector_lo(self, eng, banks):
        for t in range(NT):
            eng.wait_ge(self.hi_done, t + 1)
            hi = self.hi[:, :, t * P:(t + 1) * P]
            eng.scalar_tensor_tensor(out=self.lo[:, :, t * P:(t + 1) * P],
                                     in0=banks[t % 2][:, :].rearrange("p (k n) -> p k n", k=KT), scalar=self.scale,
                                     in1=hi.bitcast(F32) if hi.dtype == F32R else hi,
                                     op0=ALU.mult, op1=ALU.subtract).then_inc(self.lo_done, 1)

    def scalar_hi(self, eng, banks):
        for t in range(NT):
            eng.wait_ge(self.t_ready, t + 1)
            eng.activation(self.hi[:, :, t * P:(t + 1) * P], banks[t % 2][:, :].rearrange("p (k n) -> p k n", k=KT),
                           ACT.Copy, scale=self.scale).then_inc(self.hi_done, 1)

    def tensor(self, eng, banks):
        for t in range(NT):
            eng.wait_ge(self.xn_ready, t + 1)
            if t >= 2:
                eng.wait_ge(self.lo_done, t - 1)
            for k in range(KT):
                last = eng.transpose(banks[t % 2][:, k * P:(k + 1) * P], self.xn[:, t, k * P:(k + 1) * P],
                                     self.ident[:, :])
            last.then_inc(self.t_ready, 1)


def feed_forward(nc, tag, first, x, out_scale, ident, ones, const_in, x_in, weights, ternary, out):
    with ExitStack() as ctx:
        sb = lambda n, s, d=F32: ctx.enter_context(nc.sbuf_tensor(f"{n}_{tag}", s, d))
        sem = lambda n: ctx.enter_context(nc.semaphore(f"{n}_{tag}"))
        sig = lambda n, per: Signal(ctx, nc, f"{n}_{tag}", per, credit=True)
        bank = lambda n: ctx.enter_context(nc.psum_tensor(f"{n}_{tag}", [P, HALF], F32))

        x_hi, x_lo = sb("xT_hi", [P, KT, TOK], F16), sb("xT_lo", [P, KT, TOK], F16)
        q = [sb("q_gate", [P, KT, FP], F16), sb("q_up", [P, KT, FP], F16), sb("q_down", [P, FT, HID], F16)]
        q_gate, q_up, q_down = q
        inner_hi, inner_lo = sb("inner_hi", [P, FT, TOK], F16), sb("inner_lo", [P, FT, TOK], F16)
        gate, prod = sb("gate", [P, 2, HALF]), sb("prod", [P, 2, HALF])
        norm = Norm(ctx, nc, tag, x, ident, x_hi, x_lo, X_SCALE)
        t_bank = [bank("t0"), bank("t1")]
        gate_bank, up_bank = [bank("g0"), bank("g1")], [bank("u0"), bank("u1")]
        down_bank = [bank("d0"), bank("d1")]

        x_loaded, const_loaded = sem("x_loaded"), sem("const_loaded")
        w_loaded = [sem(f"w{m}_loaded") for m in range(3)]
        stored = sem("stored")
        gate_ready, up_ready = sig("gate_ready", 2), sig("up_ready", 2)
        gate_copied, prod_ready = sig("gate_copied", 2), sig("prod_ready", 2)
        inner_hi_done, inner_lo_done = sig("inner_hi_done", 2), sig("inner_lo_done", 2)
        down_ready, x_done = sig("down_ready", 2), sig("x_done", 2)

        flat = lambda a: a[:, :, :].rearrange("p a b -> p (a b)")
        NQ = 4
        CH = KT * FP // NQ
        N_W = FF * HID
        if first:
            raw = [sb(f"raw{m}", [P, KT * FP]) for m in range(3)]
            sums, total = sb("sums", [P, 3, NQ]), sb("total", [P, 3])
            above, below, mean = sb("above", [P, 3]), sb("below", [P, 3]), sb("mean", [P, 4])
            summed = [sem(f"summed{m}") for m in range(3)]
            sum_bcast, total_done, thresh = sem("sum_bcast"), sem("total_done"), sem("thresh")
            neg_done = [sem(f"neg{m}_done") for m in range(3)]
            q_done = [sem(f"q{m}_done") for m in range(3)]
            mean_done = sem("mean_done")
            sum_bank = [down_bank[0], down_bank[1], gate_bank[0]]
            ones_ready = sem("ones_ready")

        block = ctx.enter_context(nc.Block())

        @block.sync
        def _(sp):
            if first:
                sp.dma_start(ident[:, :], const_in).then_inc(const_loaded, 16)
                sp.dma_start(x[:, :, :], x_in).then_inc(x_loaded, 16)
                for m in range(3):
                    sp.dma_start(raw[m][:, :], weights[m]).then_inc(w_loaded[m], 16)
                for m in range(3):
                    sp.wait_ge(q_done[m], NQ)
                    sp.dma_start(ternary[m], flat(q[m])).then_inc(stored, 16)
                sp.wait_ge(stored, 48)
            else:
                for m in range(3):
                    sp.dma_start(flat(q[m]), ternary[m]).then_inc(w_loaded[m], 16)
                for t in range(NT):
                    sp.wait_ge(x_done.sem, x_done.now(t // 2, t % 2 + 1))
                    sp.dma_start(out[:, t, :], x[:, t, :]).then_inc(stored, 16)
                sp.wait_ge(stored, 16 * NT)

        @block.gpsimd
        def _(pool):
            norm.pool(pool)
            if first:
                for m in (1, 2):
                    pool.wait_ge(thresh, 2 * (m + 1))
                    for c in range(NQ):
                        pool.tensor_scalar(flat(q[m])[:, c * CH:(c + 1) * CH], raw[m][:, c * CH:(c + 1) * CH],
                                           below[:, m:m + 1], None, ALU.is_lt).then_inc(neg_done[m], 1)

        @block.scalar
        def _(act):
            gate_copied.start(act)
            inner_hi_done.start(act)
            if first:
                for m in range(3):
                    act.wait_ge(w_loaded[m], 16)
                    for c in range(NQ):
                        act.activation(flat(q[m])[:, c * CH:(c + 1) * CH], raw[m][:, c * CH:(c + 1) * CH], ACT.Abs,
                                       accum_out=sums[:, m, c:c + 1]).then_inc(summed[m], 1)
                    if m == 0:
                        norm.scalar_hi(act, t_bank)
            else:
                norm.scalar_hi(act, t_bank)

            with act.Fori(0, FT) as i:
                for s in range(2):
                    act.wait_ge(gate_ready.sem, gate_ready.now(i, s + 1))
                    act.wait_ge(prod_ready.sem, prod_ready.last(i, s + 1))
                    act.activation(gate[:, s, :], gate_bank[s][:, :], ACT.Copy,
                                   scale=INNER / X_SCALE ** 2).then_inc(gate_copied.sem, 1)
                for s in range(2):
                    act.wait_ge(prod_ready.sem, prod_ready.now(i, s + 1))
                    act.activation(inner_hi[:, ds(i, 1), s * HALF:(s + 1) * HALF].rearrange("p a n -> p (a n)"),
                                   prod[:, s, :], ACT.Copy).then_inc(inner_hi_done.sem, 1)

        @block.vector
        def _(dve):
            prod_ready.start(dve)
            inner_lo_done.start(dve)
            x_done.start(dve)
            if first:
                dve.memset(ones[:, :], 1.0).then_inc(ones_ready, 1)
                dve.wait_ge(x_loaded, 16)
            for t in range(NT):
                norm.vector_stats(dve, t)
            norm.vector_norm(dve)
            norm.vector_lo(dve, t_bank)
            if first:
                for m in range(3):
                    dve.wait_ge(sum_bcast, m + 1)
                    dve.reduce_sum(total[:, m:m + 1], sum_bank[m][:, 0:NQ], AX).then_inc(total_done, 1)
                    dve.wait_ge(total_done, m + 1)
                    dve.tensor_scalar(above[:, m:m + 1], total[:, m:m + 1], 0.5 / N_W, 0.5 * EPS,
                                      ALU.mult, ALU.add).then_inc(thresh, 1)
                    dve.tensor_scalar(below[:, m:m + 1], total[:, m:m + 1], -0.5 / N_W, -0.5 * EPS,
                                      ALU.mult, ALU.add).then_inc(thresh, 1)
                    dve.tensor_scalar(mean[:, m:m + 1], total[:, m:m + 1], 1.0 / N_W, None,
                                      ALU.mult).then_inc(mean_done, 1)
                    if m == 0:
                        dve.wait_ge(thresh, 2)
                        for c in range(NQ):
                            dve.tensor_scalar(flat(q[m])[:, c * CH:(c + 1) * CH], raw[m][:, c * CH:(c + 1) * CH],
                                              below[:, m:m + 1], None, ALU.is_lt).then_inc(neg_done[m], 1)
                    dve.wait_ge(thresh, 2 * (m + 1))
                    for c in range(NQ):
                        dve.wait_ge(neg_done[m], c + 1)
                        part = flat(q[m])[:, c * CH:(c + 1) * CH]
                        dve.scalar_tensor_tensor(out=part, in0=raw[m][:, c * CH:(c + 1) * CH],
                                                 scalar=above[:, m:m + 1], in1=part,
                                                 op0=ALU.is_gt, op1=ALU.subtract).then_inc(q_done[m], 1)
                dve.wait_ge(mean_done, 3)
                dve.tensor_scalar(mean[:, 3:4], mean[:, 0:1], mean[:, 1:2], mean[:, 2:3],
                                  ALU.mult, ALU.mult).then_inc(mean_done, 1)
                dve.wait_ge(mean_done, 4)
                dve.tensor_scalar(out_scale[:, :], mean[:, 3:4], 0.5 / INNER, None, ALU.mult).then_inc(mean_done, 1)
                dve.wait_ge(mean_done, 5)

            with dve.Fori(0, FT) as i:
                for s in range(2):
                    dve.wait_ge(gate_copied.sem, gate_copied.now(i, s + 1))
                    dve.wait_ge(up_ready.sem, up_ready.now(i, s + 1))
                    dve.wait_ge(inner_hi_done.sem, inner_hi_done.last(i, s + 1))
                    dve.wait_ge(inner_lo_done.sem, inner_lo_done.last(i, s + 1))
                    dve.tensor_tensor(prod[:, s, :], up_bank[s][:, :], gate[:, s, :],
                                      ALU.mult).then_inc(prod_ready.sem, 1)
                for s in range(2):
                    dve.wait_ge(inner_hi_done.sem, inner_hi_done.now(i, s + 1))
                    part = (slice(None), ds(i, 1), slice(s * HALF, (s + 1) * HALF))
                    dve.tensor_tensor(inner_lo[part].rearrange("p a n -> p (a n)"), prod[:, s, :],
                                      inner_hi[part].rearrange("p a n -> p (a n)"),
                                      ALU.subtract).then_inc(inner_lo_done.sem, 1)
            with dve.Fori(0, NT // 2) as i:
                for j in range(2):
                    dve.wait_ge(down_ready.sem, down_ready.now(i, j + 1))
                    xt = x[:, ds(2 * i + j, 1), :].rearrange("p a n -> p (a n)")
                    dve.scalar_tensor_tensor(out=xt, in0=down_bank[j][:, :], scalar=out_scale[:, 0:1], in1=xt,
                                             op0=ALU.mult, op1=ALU.add).then_inc(x_done.sem, 1)

        @block.tensor
        def _(pe):
            gate_ready.start(pe)
            up_ready.start(pe)
            down_ready.start(pe)
            if first:
                pe.wait_ge(const_loaded, 16)
                pe.wait_ge(ones_ready, 1)
            norm.tensor(pe, t_bank)
            if first:
                for m in range(3):
                    pe.wait_ge(summed[m], NQ)
                    pe.matmul(sum_bank[m][:, 0:NQ], ones[:, :], sums[:, m, :], start=True,
                              stop=True).then_inc(sum_bcast, 1)
                pe.wait_ge(total_done, 3)
                for m in range(2):
                    pe.wait_ge(q_done[m], NQ)
            else:
                for m in range(2):
                    pe.wait_ge(w_loaded[m], 16)
            pe.wait_ge(norm.lo_done, NT)

            with pe.Fori(0, FT) as i:
                for s in range(2):
                    cols = slice(s * HALF, (s + 1) * HALF)
                    for w, banks, ready, freed in ((q_gate, gate_bank, gate_ready, gate_copied),
                                                   (q_up, up_bank, up_ready, prod_ready)):
                        pe.wait_ge(freed.sem, freed.last(i, s + 1))
                        for k in range(KT):
                            for part, xs in enumerate((x_hi, x_lo)):
                                last = pe.matmul(banks[s][:, :], w[:, k, ds(i * P, P)], xs[:, k, cols],
                                                 start=k + part == 0, stop=k == KT - 1 and part == 1)
                        last.then_inc(ready.sem, 1)

            if first:
                pe.wait_ge(q_done[2], NQ)
            else:
                pe.wait_ge(w_loaded[2], 16)
            pe.wait_ge(inner_lo_done.sem, inner_lo_done.now(FT - 1, 2))
            pe.wait_ge(inner_hi_done.sem, inner_hi_done.now(FT - 1, 2))
            with pe.Fori(0, NT // 2) as i:
                for j in range(2):
                    pe.wait_ge(x_done.sem, x_done.last(i, j + 1))
                    for f in range(FT):
                        for part, inner in enumerate((inner_hi, inner_lo)):
                            last = pe.matmul(down_bank[j][:, :], inner[:, f, ds((2 * i + j) * P, P)], q_down[:, f, :],
                                             start=f + part == 0, stop=f == FT - 1 and part == 1)
                    last.then_inc(down_ready.sem, 1)


def attention_inputs(nc, x, ident, ones, x_hi, x_lo, stats, tri_in, w_v_in, w_in_in, dt_bias_in, a_log_in,
                     v_dram, g_dram):
    with ExitStack() as ctx:
        sb = lambda n, s, d=F32: ctx.enter_context(nc.sbuf_tensor(n, s, d))
        sem = lambda n: ctx.enter_context(nc.semaphore(n))
        bank = lambda n: ctx.enter_context(nc.psum_tensor(n, [P, HALF], F32))
        tri = sb("tri", [P, P])
        wv_raw, wv_hi, wv_lo = sb("wv_raw", [P, KT, KVH * D]), sb("wv_hi", [P, KT, KVH * D], F32R), \
            sb("wv_lo", [P, KT, KVH * D], F32R)
        win_raw, win_hi, win_lo = sb("win_raw", [P, KT, H]), sb("win_hi", [P, KT, P], F32R), \
            sb("win_lo", [P, KT, P], F32R)
        dt_bias, a_log = sb("dt_bias", [H, 1]), sb("a_log", [P, NT * H])
        v = sb("v_all", [P, NT, KVH * D])
        pre_t, g_t = sb("pre_t", [H, TOK]), sb("g_t", [H, TOK])
        wide = lambda n: sb(n, [P, NT * H])
        pre, mag, e, u, ln_u, d, rest, ru, corr, pos, a, g, G = map(
            wide, "pre mag expo one_plus ln_u back rest recip corr pos a_exp g cum".split())
        norm = Norm(ctx, nc, "attn", x, ident, x_hi, x_lo, 1.0)
        t_bank = [bank("at0"), bank("at1")]
        v_bank = [bank("v0"), bank("v1")]
        b = [bank(f"small{n}") for n in range(4)]

        loaded = {n: sem(f"{n}_loaded") for n in ("tri", "wv", "win", "bias", "alog")}
        cleared = sem("win_cleared")
        split_hi, split_lo = sem("split_hi"), sem("split_lo")
        pre_ready, pre_copied, nat_ready, step = sem("pre_ready"), sem("pre_copied"), sem("nat_ready"), sem("dt_step")
        act_step = sem("dt_act_step")
        cum_ready, cum_copied, gt_ready, gt_copied = sem("cum_ready"), sem("cum_copied"), sem("gt_ready"), \
            sem("gt_copied")
        v_ready, v_copied, stored = sem("v_ready"), sem("v_copied"), sem("vg_stored")
        dt_out = stats[:, 0:NT, :].rearrange("p t h -> p (t h)")
        block = ctx.enter_context(nc.Block())

        @block.sync
        def _(sp):
            sp.dma_start(tri[:, :], tri_in).then_inc(loaded["tri"], 16)
            sp.dma_start(win_raw[:, :, :], w_in_in).then_inc(loaded["win"], 16)
            sp.dma_start(wv_raw[:, :, :], w_v_in).then_inc(loaded["wv"], 16)
            sp.dma_start(dt_bias[:, :], dt_bias_in).then_inc(loaded["bias"], 16)
            sp.dma_start(a_log[:, :], a_log_in.partition_broadcast(P)).then_inc(loaded["alog"], 16)
            sp.wait_ge(gt_copied, 2)
            sp.dma_start(g_dram, g_t[:, :]).then_inc(stored, 16)
            for n in range(2 * NT):
                t, s = n // 2, n % 2
                sp.wait_ge(v_copied, n + 1)
                sp.dma_start(v_dram[4 * s:4 * s + 4, :, t, :].rearrange("g p e -> p g e"),
                             v[:, t, s * HALF:(s + 1) * HALF].rearrange("p (g e) -> p g e", g=4)).then_inc(stored, 16)
            sp.wait_ge(stored, 16 * (1 + 2 * NT))

        @block.gpsimd
        def _(pool):
            for m in (win_hi, win_lo):
                pool.memset(m[:, :, :].bitcast(F32), 0.0).then_inc(cleared, 1)
            norm.pool(pool)
            pool.wait_ge(split_hi, 1)
            pool.wait_ge(cleared, 2)
            pool.tensor_tensor(win_lo[:, :, 0:H], win_raw[:, :, :], win_hi[:, :, 0:H].bitcast(F32),
                               ALU.subtract).then_inc(split_lo, 1)
            for k in range(KT):
                pool.wait_ge(split_hi, k + 2)
                pool.tensor_tensor(wv_lo[:, k, :], wv_raw[:, k, :], wv_hi[:, k, :].bitcast(F32),
                                   ALU.subtract).then_inc(split_lo, 1)

        @block.scalar
        def _(act):
            act.wait_ge(loaded["win"], 16)
            act.wait_ge(cleared, 2)
            act.activation(win_hi[:, :, 0:H], win_raw[:, :, :], ACT.Copy).then_inc(split_hi, 1)
            act.wait_ge(loaded["wv"], 16)
            for k in range(KT):
                act.activation(wv_hi[:, k, :], wv_raw[:, k, :], ACT.Copy).then_inc(split_hi, 1)
            norm.scalar_hi(act, t_bank)
            act.wait_ge(loaded["bias"], 16)
            for s in range(2):
                act.wait_ge(pre_ready, s + 1)
                act.activation(pre_t[:, s * HALF:(s + 1) * HALF], b[s][0:H, :], ACT.Identity,
                               bias=dt_bias[:, 0:1]).then_inc(pre_copied, 1)

            def v_copy(n):
                t, s = n // 2, n % 2
                act.wait_ge(v_ready, n + 1)
                act.activation(v[:, t, s * HALF:(s + 1) * HALF], v_bank[n % 2][:, :], ACT.Copy).then_inc(v_copied, 1)

            act.wait_ge(step, 1)
            act.activation(mag[:, :], pre[:, :], ACT.Abs).then_inc(act_step, 1)
            act.wait_ge(act_step, 1)
            act.activation(e[:, :], mag[:, :], ACT.Exp, scale=-1.0).then_inc(act_step, 1)
            act.wait_ge(loaded["alog"], 16)
            act.activation(a[:, :], a_log[:, :], ACT.Exp).then_inc(act_step, 1)
            act.wait_ge(step, 2)
            act.activation(ln_u[:, :], u[:, :], ACT.Ln).then_inc(act_step, 1)
            v_copy(0)
            v_copy(1)
            act.wait_ge(cum_ready, 1)
            act.activation(G[:, :], b[0][:, 0:NT * H], ACT.Copy).then_inc(cum_copied, 1)
            v_copy(2)
            v_copy(3)
            for s in range(2):
                act.wait_ge(gt_ready, s + 1)
                act.activation(g_t[:, s * HALF:(s + 1) * HALF], b[2 + s][0:H, :], ACT.Copy).then_inc(gt_copied, 1)
            for n in range(4, 2 * NT):
                v_copy(n)

        @block.vector
        def _(dve):
            for t in range(NT):
                norm.vector_stats(dve, t)
            norm.vector_norm(dve)
            norm.vector_lo(dve, t_bank)
            done = [0]

            def own(ins):
                done[0] += 1
                ins.then_inc(step, 1)
                dve.wait_ge(step, done[0])

            dve.wait_ge(nat_ready, 1)
            own(dve.tensor_copy(pre[:, :], b[2][:, 0:NT * H]))
            dve.wait_ge(act_step, 2)
            own(dve.tensor_scalar(u[:, :], e[:, :], 1.0, None, ALU.add))
            own(dve.tensor_scalar(d[:, :], u[:, :], -1.0, None, ALU.add))
            own(dve.tensor_tensor(rest[:, :], e[:, :], d[:, :], ALU.subtract))
            own(dve.reciprocal(ru[:, :], u[:, :]))
            own(dve.tensor_tensor(corr[:, :], rest[:, :], ru[:, :], ALU.mult))
            own(dve.scalar_tensor_tensor(out=pos[:, :], in0=pre[:, :], scalar=0.0, in1=corr[:, :],
                                         op0=ALU.max, op1=ALU.add))
            dve.wait_ge(act_step, 4)
            own(dve.tensor_tensor(dt_out, pos[:, :], ln_u[:, :], ALU.add))
            own(dve.scalar_tensor_tensor(out=g[:, :], in0=dt_out, scalar=-1.0, in1=a[:, :],
                                         op0=ALU.mult, op1=ALU.mult))
            dve.wait_ge(cum_copied, 1)
            own(dve.tensor_scalar(stats[:, NT:2 * NT, :].rearrange("p t h -> p (t h)"), G[:, :], -1.0, None, ALU.mult))
            dve.wait_ge(cum_ready, 2)
            first_chunks = lambda m: m.rearrange("p (b c h) -> p b c h", b=B, c=2)[:, :, 0, :]
            own(dve.tensor_tensor(stats[:, 2 * NT:2 * NT + B, :], first_chunks(b[1][:, 0:NT * H]),
                                  first_chunks(G[:, :]), ALU.subtract))

        @block.tensor
        def _(pe):
            norm.tensor(pe, t_bank)
            pe.wait_ge(norm.lo_done, NT)
            pe.wait_ge(split_hi, 1)
            pe.wait_ge(split_lo, 1)
            for s in range(2):
                cols = slice(s * HALF, (s + 1) * HALF)
                for k in range(KT):
                    for n, (w, xs) in enumerate(((win_hi, x_hi), (win_hi, x_lo), (win_lo, x_hi))):
                        last = pe.matmul(b[s][:, :], w[:, k, :], xs[:, k, cols], start=k + n == 0,
                                         stop=k == KT - 1 and n == 2)
                last.then_inc(pre_ready, 1)
            pe.wait_ge(pre_copied, 2)
            for t in range(NT):
                last = pe.transpose(b[2][:, t * H:(t + 1) * H], pre_t[:, t * P:(t + 1) * P], ident[0:H, 0:H])
            last.then_inc(nat_ready, 1)

            def project_v(n):
                t, s = n // 2, n % 2
                if n >= 2:
                    pe.wait_ge(v_copied, n - 1)
                for k in range(KT):
                    for m, (xs, w) in enumerate(((x_hi, wv_hi), (x_lo, wv_hi), (x_hi, wv_lo))):
                        last = pe.matmul(v_bank[n % 2][:, :], xs[:, k, t * P:(t + 1) * P],
                                         w[:, k, s * HALF:(s + 1) * HALF], start=k + m == 0,
                                         stop=k == KT - 1 and m == 2)
                last.then_inc(v_ready, 1)

            pe.wait_ge(split_hi, 1 + KT)
            pe.wait_ge(split_lo, 1 + KT)
            project_v(0)
            project_v(1)
            pe.wait_ge(loaded["tri"], 16)
            pe.wait_ge(step, 9)
            pe.matmul(b[0][:, 0:NT * H], tri[:, :], g[:, :], start=True, stop=True).then_inc(cum_ready, 1)
            pe.matmul(b[1][:, 0:NT * H], ones[:, :], g[:, :], start=True, stop=True).then_inc(cum_ready, 1)
            project_v(2)
            pe.wait_ge(cum_copied, 1)
            for s in range(2):
                for t in range(4):
                    tt = 4 * s + t
                    last = pe.transpose(b[2 + s][0:H, t * P:(t + 1) * P], G[:, tt * H:(tt + 1) * H], ident[:, :])
                last.then_inc(gt_ready, 1)
            for n in range(3, 2 * NT):
                project_v(n)




def steps(text):
    return [(s[0], int(s[1:])) for s in text.split()]


ORDER = {
    "tensor": steps(
        "R0 R1 R2 R3 G0 R4 R5 G1 R6 S0 S1 R7 Y0 S2 S3 R8 R9 T0 Y1 G2 G3 Y2 S4 S5 T1 G4 S6 S7 Y3 S8 O0 S9 S10 "
        "Y4 O1 T2 G5 Y5 G6 T3 G7 Y6 T4 S11 O2 O3 T5 Y7 O4 T6 O5 T7 O6 O7"),
    "scalar": steps(
        "W0 W1 W2 R0 R1 R2 R3 E0 R4 R5 E1 E2 E3 G0 G1 R6 W3 R7 Y0 E4 R8 R9 Y1 T0 E5 E6 E7 G2 Y2 G3 G4 E8 T1 "
        "Y3 Y4 E9 E10 G5 T2 Y5 E11 T3 G6 G7 Y6 T4 T5 Y7 T6 T7"),
    "vector": steps(
        "W1 H0 C0 C1 A0 A1 C2 A2 C3 A3 C4 C5 A4 A5 G0 P0 P1 C6 P2 C7 Y0 A6 A7 P3 C8 G1 C9 A8 A9 Y1 T0 G2 P4 "
        "P5 Y2 G3 P6 G4 P7 P8 T1 Y3 X0 X1 Y4 T2 G5 P9 Y5 T3 G6 G7 P10 P11 Y6 T4 X2 T5 X3 X4 Y7 T6 X5 T7 X6 X7"),
    "gpsimd": steps(
        "W0 W2 R0 R1 R2 M0 R3 M1 M2 R4 R5 R6 R7 Y0 M3 M4 R8 R9 Y1 W3 Y2 M5 M6 Y3 Y4 M7 Y5 Y6 Y7"),
}
NR = 2 + 2 * REP
SHARED = [p for p in ORDER["tensor"] if p[0] in "GO"]
BLOCKS = ((0, 0), (0, 1), (1, 1))


def attention(nc, x, ident, x_hi, x_lo, stats, w_q_in, w_k_in, w_g_in, w_o_in, table_in, gnorm_in, v_dram, g_dram):
    with ExitStack() as ctx:
        sb = lambda n, s, d=F32: ctx.enter_context(nc.sbuf_tensor(n, s, d))
        sem = lambda n: ctx.enter_context(nc.semaphore(n))
        sig = lambda n, per: Signal(ctx, nc, n, per, credit=True)
        bank = lambda n: ctx.enter_context(nc.psum_tensor(n, [P, HALF], F32))

        cos, sin, mask = sb("cos", [P, HALF]), sb("sin_signed", [P, HALF]), sb("causal_mask", [P, HALF])
        gnorm, eps4, power = sb("gnorm", [P, 1]), sb("eps4", [P, REP]), sb("neg_half", [P, REP])
        raw_k, raw_g = sb("raw_k", [P, KT, D]), sb("raw_g", [P, KT, HALF])
        raw_qo = sb("raw_qo", [P, KT, HALF])
        w = {n: (sb(f"w{n}_hi", [P, KT, D if n == "k" else HALF], F32R),
                 sb(f"w{n}_lo", [P, KT, D if n == "k" else HALF], F32R)) for n in "kqgo"}
        raw = {"k": raw_k, "q": raw_qo, "g": raw_g, "o": raw_qo}
        k_t, q_t = sb("k_t", [P, TOK]), sb("q_t", [P, REP, TOK])
        v = sb("v", [P, NT, D])
        g_rows = sb("g_rows", [P, 2, REP, L])
        g_masked = sb("g_masked", [P, REP, P])
        prob = sb("prob", [P, 2, len(BLOCKS), REP, P])
        rot_a, rot_b = sb("rot_cos", [P, 2, HALF]), sb("rot_sin", [P, 2, HALF])
        z = sb("z", [P, 4, REP, D])
        z_hi, z_lo = sb("z_t_hi", [P, 2, REP, P], F32R), sb("z_t_lo", [P, 2, REP, P], F32R)
        junk = sb("squares", [P, REP, D], F16)
        sumsq, sum_eps, rinv = sb("sumsq", [P, NT, REP]), sb("sum_eps", [P, NT, REP]), sb("rinv", [P, NT, REP])
        head = sb("head_stats", [P, 2 * NT + B, REP])
        rot_bank, mul_bank, s_bank = [bank("r0"), bank("r1")], [bank("j0"), bank("j1")], [bank("s0"), bank("s1")]
        y_bank, z_bank = bank("y"), bank("zt")

        table_loaded, consts_ready = sem("table_loaded"), sem("attn_consts")
        ld_k, ld_g, ld_v = (Signal(ctx, nc, f"load_{n}", 16) for n in "kgv")
        ld_qo = Signal(ctx, nc, "load_qo", 32)
        ld_rows = [Signal(ctx, nc, f"load_rows{n}", 32) for n in range(2)]
        hi_done = sig("w_hi_done", 4)
        lo_done, q_lo_done = sig("w_lo_done", 3), sig("wq_lo_done", 1)
        rot_ready, cos_done, swap_done = sig("rot_ready", NR), sig("cos_done", NR), sig("swap_done", NR)
        sin_done, rot_done = sig("sin_done", NR), sig("rot_done", NR)
        mul_ready = sig("mul_ready", len(SHARED))
        tanh_done, silu_done, x_added = sig("tanh_done", NT), sig("silu_done", NT), sig("x_added", NT)
        mask_done, decay_done = sig("mask_done", 2 * B), sig("decay_done", 3 * B)
        score_ready, prob_done = sig("score_ready", 3 * B), sig("prob_done", 3 * B)
        y_ready, square_done, eps_done, rinv_done = (sig(n, NT) for n in ("y_ready", "square_done", "eps_done",
                                                                         "rinv_done"))
        z_done, zt_ready, zhi_done, zlo_done = (sig(n, NT) for n in ("z_done", "zt_ready", "zhi_done", "zlo_done"))
        head_copied = sig("head_copied", 1)

        def used(sg, g, n, ring):
            return sg.now(g, n - ring + 1) if n >= ring else sg.last(g, sg.per + n - ring + 1)

        def mul_at(what, t):
            return SHARED.index((what, t))

        block = ctx.enter_context(nc.Block())

        @block.sync
        def _(sp):
            for n, m in enumerate((cos, sin, mask)):
                sp.dma_start(m[:, :], table_in[:, n, :]).then_inc(table_loaded, 16)
            sp.dma_start(gnorm[:, :], gnorm_in).then_inc(table_loaded, 16)
            with sp.Fori(0, KVH) as g:
                pick = lambda a: a[ds(g, 1), :, :, :].rearrange("a p k n -> (a p) k n")
                sp.wait_ge(lo_done.sem, lo_done.last(g, 1))
                sp.dma_start(raw_k[:, :, :], pick(w_k_in)).then_inc(ld_k.sem, 16)
                sp.wait_ge(lo_done.sem, lo_done.last(g, 3))
                sp.dma_start(raw_qo[:, :, :], pick(w_q_in)).then_inc(ld_qo.sem, 16)
                sp.dma_start(raw_g[:, :, :], pick(w_g_in)).then_inc(ld_g.sem, 16)
                sp.wait_ge(q_lo_done.sem, q_lo_done.now(g, 1))
                sp.dma_start(raw_qo[:, :, :], pick(w_o_in)).then_inc(ld_qo.sem, 16)
                sp.wait_ge(y_ready.sem, y_ready.last(g, NT))
                sp.dma_start(v[:, :, :], pick(v_dram)).then_inc(ld_v.sem, 16)
                for b in range(B):
                    sp.wait_ge(decay_done.sem, decay_done.now(g, 3 * (b - 1)) if b >= 2 else
                               decay_done.last(g, 3 * (B + b - 1)))
                    sp.dma_start(g_rows[:, b % 2, :, :],
                                 g_dram[ds(g * REP, REP), b * L:(b + 1) * L].partition_broadcast(P)
                                 ).then_inc(ld_rows[b % 2].sem, 16)

        @block.gpsimd
        def _(pool):
            for sg in (lo_done, sin_done, mask_done, eps_done, rinv_done):
                sg.start(pool)
            pool.memset(eps4[:, :], 4 * EPS).then_inc(consts_ready, 1)
            pool.memset(power[:, :], -0.5).then_inc(consts_ready, 1)
            pool.wait_ge(consts_ready, 2)
            pool.wait_ge(table_loaded, 64)
            with pool.Fori(0, KVH) as g:

                def split_lo(n):
                    name = "kqgo"[n]
                    pool.wait_ge(hi_done.sem, hi_done.now(g, n + 1))
                    pool.tensor_tensor(w[name][1][:, :, :], raw[name][:, :, :], w[name][0][:, :, :].bitcast(F32),
                                       ALU.subtract).then_inc(lo_done.sem, 1)

                for what, n in ORDER["gpsimd"]:
                    if what == "W":
                        split_lo(n)
                    elif what == "R":
                        pool.wait_ge(swap_done.sem, swap_done.now(g, n + 1))
                        pool.tensor_tensor(rot_b[:, n % 2, :], rot_b[:, n % 2, :], sin[:, :],
                                           ALU.mult).then_inc(sin_done.sem, 1)
                    elif what == "M":
                        b, chunk = n // 2, n % 2
                        rows = g_rows[:, b % 2, :, chunk * P:(chunk + 1) * P]
                        causal = mask[:, :].rearrange("p (h i) -> p h i", h=REP)
                        pool.wait_ge(ld_rows[b % 2].sem, ld_rows[b % 2].now(g, 16 * (b // 2 + 1)))
                        if chunk:
                            pool.wait_ge(decay_done.sem, decay_done.now(g, 3 * b) if b else decay_done.last(g, 3 * B))
                            masked = g_masked[:, :, :]
                        else:
                            masked = rows
                        pool.tensor_tensor(masked, rows, causal, ALU.add).then_inc(mask_done.sem, 1)
                    elif what == "Y":
                        pool.wait_ge(square_done.sem, square_done.now(g, n + 1))
                        pool.tensor_tensor(sum_eps[:, n, :], sumsq[:, n, :], eps4[:, :], ALU.add).then_inc(eps_done.sem, 1)
                        pool.wait_ge(eps_done.sem, eps_done.now(g, n + 1))
                        pool.tensor_tensor(rinv[:, n, :], sum_eps[:, n, :], power[:, :], ALU.pow).then_inc(rinv_done.sem, 1)

        @block.scalar
        def _(act):
            for sg in (hi_done, swap_done, tanh_done, decay_done, square_done, zhi_done):
                sg.start(act)
            act.wait_ge(table_loaded, 64)
            with act.Fori(0, KVH) as g:

                def split_hi(n):
                    name = "kqgo"[n]
                    loaded, count = ((ld_k, 16), (ld_qo, 16), (ld_g, 16), (ld_qo, 32))[n]
                    act.wait_ge(loaded.sem, loaded.now(g, count))
                    user, k = ((rot_ready, 2), (rot_ready, NR), (mul_ready, mul_at("G", NT - 1) + 1),
                               (mul_ready, len(SHARED)))[n]
                    act.wait_ge(user.sem, user.last(g, k))
                    act.activation(w[name][0][:, :, :], raw[name][:, :, :], ACT.Copy).then_inc(hi_done.sem, 1)

                for what, n in ORDER["scalar"]:
                    if what == "W":
                        split_hi(n)
                    elif what == "R":
                        act.wait_ge(rot_ready.sem, rot_ready.now(g, n + 1))
                        act.wait_ge(rot_done.sem, used(rot_done, g, n, 2))
                        act.activation(rot_b[0:64, n % 2, :], rot_bank[n % 2][64:128, :], ACT.Copy)
                        act.activation(rot_b[64:128, n % 2, :], rot_bank[n % 2][0:64, :],
                                       ACT.Copy).then_inc(swap_done.sem, 1)
                    elif what == "E":
                        b, m = n // 3, n % 3
                        if m == 0:
                            act.wait_ge(head_copied.sem, head_copied.now(g, 1))
                            act.wait_ge(y_ready.sem, used(y_ready, g, 2 * b + 1, 4))
                            act.wait_ge(mask_done.sem, mask_done.now(g, 2 * b + 1))
                        elif m == 2:
                            act.wait_ge(mask_done.sem, mask_done.now(g, 2 * b + 2))
                        for h in range(REP):
                            if m == 0:
                                rows, bias = g_rows[:, b % 2, h, 0:P], head[:, NT + 2 * b, h:h + 1]
                            elif m == 1:
                                rows, bias = g_rows[:, b % 2, h, P:L], head[:, 2 * NT + b, h:h + 1]
                            else:
                                rows, bias = g_masked[:, h, :], head[:, NT + 2 * b + 1, h:h + 1]
                            last = act.activation(prob[:, b % 2, m, h, :], rows, ACT.Exp, bias=bias)
                        last.then_inc(decay_done.sem, 1)
                    elif what == "G":
                        m = mul_at("G", n)
                        act.wait_ge(mul_ready.sem, mul_ready.now(g, m + 1))
                        act.wait_ge(zt_ready.sem, used(zt_ready, g, n, 4))
                        act.activation(z[:, n % 4, :, :].rearrange("p h e -> p (h e)"), mul_bank[m % 2][:, :], ACT.Tanh,
                                       scale=0.5).then_inc(tanh_done.sem, 1)
                    elif what == "Y":
                        act.wait_ge(y_ready.sem, y_ready.now(g, n + 1))
                        act.wait_ge(square_done.sem, used(square_done, g, n, 1))
                        for h in range(REP):
                            last = act.activation(junk[:, h, :], y_bank[:, h * D:(h + 1) * D], ACT.Square,
                                                  scale=(4.0 / D) ** 0.5, accum_out=sumsq[:, n, h:h + 1])
                        last.then_inc(square_done.sem, 1)
                    elif what == "T":
                        act.wait_ge(zt_ready.sem, zt_ready.now(g, n + 1))
                        o = mul_at("O", (n - 2) % NT) + 1
                        act.wait_ge(mul_ready.sem, mul_ready.now(g, o) if n >= 2 else mul_ready.last(g, o))
                        act.activation(z_hi[:, n % 2, :, :].rearrange("p h i -> p (h i)"), z_bank[:, :], ACT.Copy,
                                       scale=gnorm[:, 0:1]).then_inc(zhi_done.sem, 1)

        @block.vector
        def _(dve):
            for sg in (q_lo_done, cos_done, rot_done, silu_done, prob_done, z_done, zlo_done, x_added, head_copied):
                sg.start(dve)
            dve.wait_ge(table_loaded, 64)
            with dve.Fori(0, KVH) as g:
                for what, n in ORDER["vector"]:
                    if what == "H":
                        dve.wait_ge(decay_done.sem, decay_done.last(g, 3 * B))
                        dve.wait_ge(prob_done.sem, prob_done.last(g, 3 * B))
                        dve.tensor_copy(head[:, :, :], stats[:, :, ds(g * REP, REP)]).then_inc(head_copied.sem, 1)
                    elif what == "W":
                        dve.wait_ge(hi_done.sem, hi_done.now(g, 2))
                        dve.tensor_tensor(w["q"][1][:, :, :], raw_qo[:, :, :], w["q"][0][:, :, :].bitcast(F32),
                                          ALU.subtract).then_inc(q_lo_done.sem, 1)
                    elif what == "C":
                        dve.wait_ge(swap_done.sem, swap_done.now(g, n + 1))
                        dve.wait_ge(rot_done.sem, used(rot_done, g, n, 2))
                        dve.tensor_tensor(rot_a[:, n % 2, :], rot_bank[n % 2][:, :], cos[:, :],
                                          ALU.mult).then_inc(cos_done.sem, 1)
                    elif what == "A":
                        dve.wait_ge(sin_done.sem, sin_done.now(g, n + 1))
                        dve.wait_ge(cos_done.sem, cos_done.now(g, n + 1))
                        if n == 0:
                            dve.wait_ge(score_ready.sem, score_ready.last(g, 3 * B))
                        if n < 2:
                            dst = k_t[:, n * HALF:(n + 1) * HALF]
                        else:
                            s, h = (n - 2) // REP, (n - 2) % REP
                            dst = q_t[:, h, s * HALF:(s + 1) * HALF]
                        dve.tensor_tensor(dst, rot_a[:, n % 2, :], rot_b[:, n % 2, :], ALU.add).then_inc(rot_done.sem, 1)
                    elif what == "P":
                        b, (kc, qc) = n // 3, BLOCKS[n % 3]
                        dve.wait_ge(head_copied.sem, head_copied.now(g, 1))
                        dve.wait_ge(score_ready.sem, score_ready.now(g, n + 1))
                        dve.wait_ge(decay_done.sem, decay_done.now(g, n + 1))
                        for h in range(REP):
                            p = prob[:, b % 2, n % 3, h, :]
                            last = dve.scalar_tensor_tensor(out=p, in0=s_bank[n % 2][:, h * P:(h + 1) * P],
                                                            scalar=head[:, 2 * b + kc, h:h + 1], in1=p,
                                                            op0=ALU.mult, op1=ALU.mult)
                        last.then_inc(prob_done.sem, 1)
                    elif what == "G":
                        m = mul_at("G", n)
                        zt = z[:, n % 4, :, :].rearrange("p h e -> p (h e)")
                        dve.wait_ge(tanh_done.sem, tanh_done.now(g, n + 1))
                        dve.scalar_tensor_tensor(out=zt, in0=zt, scalar=1.0, in1=mul_bank[m % 2][:, :],
                                                 op0=ALU.add, op1=ALU.mult).then_inc(silu_done.sem, 1)
                    elif what == "Y":
                        dve.wait_ge(rinv_done.sem, rinv_done.now(g, n + 1))
                        dve.wait_ge(silu_done.sem, silu_done.now(g, n + 1))
                        for h in range(REP):
                            zt = z[:, n % 4, h, :]
                            last = dve.scalar_tensor_tensor(out=zt, in0=y_bank[:, h * D:(h + 1) * D],
                                                            scalar=rinv[:, n, h:h + 1], in1=zt,
                                                            op0=ALU.mult, op1=ALU.mult)
                        last.then_inc(z_done.sem, 1)
                    elif what == "T":
                        dve.wait_ge(zhi_done.sem, zhi_done.now(g, n + 1))
                        dve.scalar_tensor_tensor(out=z_lo[:, n % 2, :, :].rearrange("p h i -> p (h i)"),
                                                 in0=z_bank[:, :], scalar=gnorm[:, 0:1],
                                                 in1=z_hi[:, n % 2, :, :].rearrange("p h i -> p (h i)").bitcast(F32),
                                                 op0=ALU.mult, op1=ALU.subtract).then_inc(zlo_done.sem, 1)
                    elif what == "X":
                        m = mul_at("O", n)
                        dve.wait_ge(mul_ready.sem, mul_ready.now(g, m + 1))
                        dve.wait_ge(x_added.sem, x_added.last(g, n + 1))
                        dve.tensor_tensor(x[:, n, :], mul_bank[m % 2][:, :], x[:, n, :], ALU.add).then_inc(x_added.sem, 1)

        @block.tensor
        def _(pe):
            for sg in (rot_ready, mul_ready, score_ready, y_ready, zt_ready):
                sg.start(pe)

            def three_pass(out, a, b, k_range):
                for k in k_range:
                    for n, (i, j) in enumerate(((0, 0), (0, 1), (1, 0))):
                        last = pe.matmul(out, a(k)[i], b(k)[j], start=k == k_range[0] and n == 0,
                                         stop=k == k_range[-1] and n == 2)
                return last

            with pe.Fori(0, KVH) as g:

                def split_ready(n):
                    pe.wait_ge(hi_done.sem, hi_done.now(g, n + 1))
                    if n == 1:
                        pe.wait_ge(q_lo_done.sem, q_lo_done.now(g, 1))
                    else:
                        pe.wait_ge(lo_done.sem, lo_done.now(g, (1, None, 2, 3)[n]))

                def mul_free(m):
                    what, t = SHARED[(m - 2) % len(SHARED)]
                    sg = silu_done if what == "G" else x_added
                    pe.wait_ge(sg.sem, sg.now(g, t + 1) if m >= 2 else sg.last(g, t + 1))

                for what, n in ORDER["tensor"]:
                    if what == "R":
                        if n in (0, 2):
                            split_ready(0 if n == 0 else 1)
                        pe.wait_ge(cos_done.sem, used(cos_done, g, n, 2))
                        s, h = (n, 0) if n < 2 else ((n - 2) // REP, (n - 2) % REP)
                        wt, cols = w["k" if n < 2 else "q"], slice(s * HALF, (s + 1) * HALF)
                        three_pass(rot_bank[n % 2][:, :],
                                   lambda k: [m[:, k, h * D:(h + 1) * D] for m in wt],
                                   lambda k: (x_hi[:, k, cols], x_lo[:, k, cols]),
                                   range(KT)).then_inc(rot_ready.sem, 1)
                    elif what == "G":
                        if n == 0:
                            split_ready(2)
                        m = mul_at("G", n)
                        mul_free(m)
                        rows = slice(n * P, (n + 1) * P)
                        three_pass(mul_bank[m % 2][:, :], lambda k: (x_hi[:, k, rows], x_lo[:, k, rows]),
                                   lambda k: [a[:, k, :] for a in w["g"]], range(KT)).then_inc(mul_ready.sem, 1)
                    elif what == "S":
                        b, (kc, qc) = n // 3, BLOCKS[n % 3]
                        pe.wait_ge(rot_done.sem, rot_done.now(g, 2 + REP * (b // 2 + 1)))
                        pe.wait_ge(prob_done.sem, used(prob_done, g, n, 2))
                        kt, qt = 2 * b + kc, 2 * b + qc
                        pe.matmul(s_bank[n % 2][:, :], k_t[:, kt * P:(kt + 1) * P], q_t[:, :, qt * P:(qt + 1) * P],
                                  start=True, stop=True).then_inc(score_ready.sem, 1)
                    elif what == "Y":
                        b, qc = n // 2, n % 2
                        if n == 0:
                            pe.wait_ge(ld_v.sem, ld_v.now(g, 16))
                        pe.wait_ge(prob_done.sem, prob_done.now(g, 3 * b + (3 if qc else 1)))
                        pe.wait_ge(z_done.sem, used(z_done, g, n, 1))
                        mine = [(m, kc) for m, (kc, c) in enumerate(BLOCKS) if c == qc]
                        for h in range(REP):
                            for m, kc in mine:
                                last = pe.matmul(y_bank[:, h * D:(h + 1) * D], prob[:, b % 2, m, h, :],
                                                 v[:, 2 * b + kc, :], start=m == mine[0][0], stop=m == mine[-1][0])
                        last.then_inc(y_ready.sem, 1)
                    elif what == "T":
                        pe.wait_ge(z_done.sem, z_done.now(g, n + 1))
                        pe.wait_ge(zlo_done.sem, used(zlo_done, g, n, 1))
                        for h in range(REP):
                            last = pe.transpose(z_bank[:, h * P:(h + 1) * P], z[:, n % 4, h, :], ident[:, :])
                        last.then_inc(zt_ready.sem, 1)
                    elif what == "O":
                        if n == 0:
                            split_ready(3)
                        m = mul_at("O", n)
                        mul_free(m)
                        pe.wait_ge(zhi_done.sem, zhi_done.now(g, n + 1))
                        pe.wait_ge(zlo_done.sem, zlo_done.now(g, n + 1))
                        three_pass(mul_bank[m % 2][:, :], lambda h: (z_hi[:, n % 2, h, :], z_lo[:, n % 2, h, :]),
                                   lambda h: [a[:, h, :] for a in w["o"]], range(REP)).then_inc(mul_ready.sem, 1)


def build(nc, args, out):
    (x_in, w_q, w_k, w_v, w_g, w_o, w_in, dt_bias, a_log, gnorm, w_gate, w_up, w_down, squares, tables) = args
    with ExitStack() as ctx:
        sb = lambda n, s, d=F32: ctx.enter_context(nc.sbuf_tensor(n, s, d))
        x = sb("x", [P, NT, HID])
        ident, ones, out_scale = sb("ident", [P, P]), sb("ones", [P, P]), sb("out_scale", [P, 1])
        ternary = [nc.dram_tensor(f"ternary{m}", [P, KT * FP], F16, kind="Internal").ap() for m in range(3)]
        v_dram = nc.dram_tensor("v_by_head", [KVH, P, NT, D], F32, kind="Internal").ap()
        g_dram = nc.dram_tensor("g_rows_dram", [H, TOK], F32, kind="Internal").ap()
        tiles = lambda a: a.rearrange("(t p) n -> p t n", p=P)
        feed_forward(nc, "ffn1", True, x, out_scale, ident, ones, squares[:, 0, :], tiles(x_in),
                     (w_gate, w_up, w_down), ternary, None)
        with ExitStack() as inner:
            sbi = lambda n, s, d=F32: inner.enter_context(nc.sbuf_tensor(n, s, d))
            x_hi, x_lo = sbi("ax_hi", [P, KT, TOK], F32R), sbi("ax_lo", [P, KT, TOK], F32R)
            stats = sbi("stats", [P, 2 * NT + B, H])
            attention_inputs(nc, x, ident, ones, x_hi, x_lo, stats, squares[:, 1, :], w_v, w_in, dt_bias, a_log,
                             v_dram, g_dram)
            attention(nc, x, ident, x_hi, x_lo, stats, w_q, w_k, w_g, w_o, tables, gnorm, v_dram, g_dram)
        feed_forward(nc, "ffn2", False, x, out_scale, ident, ones, None, None, None, ternary, tiles(out))


def kernel(L0_attn_hidden_states, L0_attn_Wq, L0_attn_Wk, L0_attn_Wv, L0_attn_Wo, L0_attn_Wg, L0_attn_Win,
           L0_attn_dt_bias, L0_attn_A_log_bias, L0_attn_gnorm_w, L0_ffn_w_gate, L0_ffn_w_up, L0_ffn_w_down):
    import numpy as np
    import concourse.bacc as bacc
    from concourse.bass_utils import run_bass_kernel_spmd

    a = np.asarray
    by_head = lambda w: a(w).reshape(KVH, -1, KT, P).transpose(0, 3, 2, 1)
    contracted = lambda w: a(w).reshape(-1, KT, P).transpose(2, 1, 0)
    padded = np.zeros((FP - FF, HID), np.float32)
    inner_first = lambda w: np.concatenate([a(w), padded])
    gate, up = (contracted(inner_first(w)).reshape(P, KT * FP) for w in (L0_ffn_w_gate, L0_ffn_w_up))
    down = inner_first(a(L0_ffn_w_down).T).reshape(FT, P, HID).transpose(1, 0, 2).reshape(P, FT * HID)
    w_o = a(L0_attn_Wo).reshape(HID, KVH, REP, D).transpose(1, 3, 2, 0)

    i = np.arange(P)
    squares = np.stack([np.eye(P), i[:, None] <= i[None, :]], 1).astype(np.float32)
    inv_freq = (np.float32(1) / np.power(np.float32(10000), np.arange(0, D, 2, dtype=np.float32) / np.float32(D)))
    ang = (np.arange(L, dtype=np.float32)[:, None] * inv_freq.astype(np.float32)).astype(np.float64)
    cos = np.tile(np.concatenate([np.cos(ang), np.cos(ang)], 1).T, (1, HALF // L))
    sin = np.tile(np.concatenate([-np.sin(ang), np.sin(ang)], 1).T, (1, HALF // L))
    mask = np.tile(np.where(i[:, None] <= i[None, :], 0.0, -BIG), (1, REP))
    tables = np.stack([cos, sin, mask], 1).astype(np.float32)

    ins = {
        "x_in": a(L0_attn_hidden_states).reshape(TOK, HID),
        "w_q": by_head(L0_attn_Wq), "w_k": by_head(L0_attn_Wk), "w_v": contracted(L0_attn_Wv),
        "w_g": by_head(L0_attn_Wg), "w_o": w_o, "w_in": contracted(L0_attn_Win),
        "dt_bias": a(L0_attn_dt_bias).reshape(H, 1), "a_log": np.tile(a(L0_attn_A_log_bias), NT),
        "gnorm": a(L0_attn_gnorm_w).reshape(D, 1), "w_gate": gate, "w_up": up, "w_down": down,
        "squares": squares, "tables": tables,
    }
    nc = bacc.Bacc("TRN2", target_bir_lowering=False, num_devices=1)
    arrays, args = {}, []
    for name, v in ins.items():
        arrays[f"in_{name}"] = np.ascontiguousarray(v)
        args.append(nc.dram_tensor(f"in_{name}", arrays[f"in_{name}"].shape, mybir.dt.from_np(arrays[f"in_{name}"].dtype),
                                   kind="ExternalInput").ap())
    out = nc.dram_tensor("out", (TOK, HID), F32, kind="ExternalOutput").ap()
    build(nc, args, out)
    r = run_bass_kernel_spmd(nc, [arrays], core_ids=[0])
    return r.results[0]["out"].reshape(B, L, HID)
```

```python
from contextlib import ExitStack

import numpy as np

import concourse.bass as bass
from concourse import mybir
from concourse.bass import ds

P = 128
B, L, HID = 4, 256, 512
H, KVH, D = 32, 8, 128
REP = H // KVH
FF = 1376
TOK = B * L
NT = TOK // P
KT = HID // P
FT = -(-FF // P)
FP = FT * P
HALF = 512
EPS = 1e-5
BIG = 1e30

ALU = mybir.AluOpType
ACT = mybir.ActivationFunctionType
F32, F32R, F16 = mybir.dt.float32, mybir.dt.float32r, mybir.dt.float16
AX = mybir.AxisListType.X

X_SCALE = 2048.0
INNER = 2.0 ** -3


class Signal:

    def __init__(self, ctx, nc, name, per=1, credit=False):
        self.sem, self.per, self.credit = ctx.enter_context(nc.semaphore(name)), per, credit

    def start(self, eng):
        if self.credit:
            eng.sem_inc(self.sem, self.per)

    def now(self, g, k):
        return (g + int(self.credit)) * self.per + k

    def last(self, g, k):
        assert self.credit and not (isinstance(k, int) and k < 1)
        return g * self.per + k


class Arena:

    def __init__(self, nc, base):
        self.nc, self.base = nc, base

    def __call__(self, name, shape, dtype, offset):
        return self.nc.alloc_sbuf_tensor_at(name, shape, dtype, offset=self.base + offset)

    def between(self, spans):
        free = [list(span) for span in spans]

        def put(name, shape, dtype=F32):
            size = int(np.prod(shape[1:])) * (2 if dtype == F16 else 4)
            for span in free:
                if span[0] + size <= span[1]:
                    span[0] += -(-size // 32) * 32
                    return self(name, shape, dtype, span[0] - -(-size // 32) * 32)
            raise ValueError(f"no room for {name}")

        return put


HEADSTART = NT // 2


class Norm:

    def __init__(self, ctx, nc, tag, x, ident, hi, lo, scale, xn, banks):
        sb = lambda n, s, d=F32: ctx.enter_context(nc.sbuf_tensor(f"{n}_{tag}", s, d))
        self.x, self.ident, self.hi_t, self.lo_t, self.scale = x, ident, hi, lo, scale
        self.xn, self.banks = xn, banks
        self.parts = sb("bn_parts", [P, NT, 6])
        self.mv = sb("mean_var", [P, NT, 2])
        self.var = sb("var_eps", [P, NT])
        self.rstd = sb("rstd", [P, NT])
        self.eps = sb("eps", [P, 1])
        self.power = sb("power", [P, 1])
        sig = lambda n: Signal(ctx, nc, f"{n}_{tag}", 2, credit=True)
        self.consts = ctx.enter_context(nc.semaphore(f"ln_consts_{tag}"))
        self.stat, self.aggr, self.veps, self.rstd_ready = sig("ln_stat"), sig("ln_aggr"), sig("ln_veps"), sig("ln_rstd")
        self.xn_ready, self.t_ready, self.hi_done, self.lo_done = sig("ln_xn"), sig("ln_t"), sig("ln_hi"), sig("ln_lo")

    def start_vector(self, eng):
        for sg in (self.stat, self.aggr, self.xn_ready, self.lo_done):
            sg.start(eng)

    def start_pool(self, eng):
        self.veps.start(eng)
        self.rstd_ready.start(eng)
        eng.memset(self.eps[:, :], EPS).then_inc(self.consts, 1)
        eng.memset(self.power[:, :], -0.5).then_inc(self.consts, 1)
        eng.wait_ge(self.consts, 2)

    def stats(self, eng, t):
        eng.bn_stats(self.parts[:, t, :], self.x[:, t, :]).then_inc(self.stat.sem, 1)
        eng.wait_ge(self.stat.sem, self.stat.now(0, t + 1))
        eng.bn_aggr(self.mv[:, t, :], self.parts[:, t, :]).then_inc(self.aggr.sem, 1)

    def rsqrt(self, eng, t):
        var = self.mv[:, ds(t, 1), :].rearrange("p a n -> p (a n)")[:, 1:2]
        eng.wait_ge(self.aggr.sem, self.aggr.now(0, t + 1))
        eng.tensor_tensor(self.var[:, ds(t, 1)], var, self.eps[:, :], ALU.add).then_inc(self.veps.sem, 1)
        eng.wait_ge(self.veps.sem, self.veps.now(0, t + 1))
        eng.tensor_tensor(self.rstd[:, ds(t, 1)], self.var[:, ds(t, 1)], self.power[:, :],
                          ALU.pow).then_inc(self.rstd_ready.sem, 1)

    def normalize(self, eng, t, slot, ring):
        eng.wait_ge(self.rstd_ready.sem, self.rstd_ready.now(0, t + 1))
        if ring:
            eng.wait_ge(self.t_ready.sem, self.t_ready.now(0, t + 1 - ring))
        eng.tensor_scalar(self.xn[slot], self.x[:, ds(t, 1), :].rearrange("p a n -> p (a n)"),
                          self.mv[:, ds(t, 1), :].rearrange("p a n -> p (a n)")[:, 0:1],
                          self.rstd[:, ds(t, 1)], ALU.subtract, ALU.mult).then_inc(self.xn_ready.sem, 1)

    def transpose(self, eng, t, slot, ring):
        eng.wait_ge(self.xn_ready.sem, self.xn_ready.now(0, t + 1))
        if ring:
            eng.wait_ge(self.lo_done.sem, self.lo_done.now(0, t + 1 - ring))
        for k in range(KT):
            last = eng.transpose(self.banks[slot][:, k * P:(k + 1) * P], self.xn[slot][:, k * P:(k + 1) * P],
                                 self.ident[:, :])
        last.then_inc(self.t_ready.sem, 1)

    def hi(self, eng, t, slot):
        eng.wait_ge(self.t_ready.sem, self.t_ready.now(0, t + 1))
        eng.activation(self.hi_t[:, :, ds(t * P, P)], self.banks[slot][:, :].rearrange("p (k n) -> p k n", k=KT),
                       ACT.Copy, scale=self.scale).then_inc(self.hi_done.sem, 1)

    def lo(self, eng, t, slot):
        eng.wait_ge(self.hi_done.sem, self.hi_done.now(0, t + 1))
        hi = self.hi_t[:, :, ds(t * P, P)]
        eng.scalar_tensor_tensor(out=self.lo_t[:, :, ds(t * P, P)],
                                 in0=self.banks[slot][:, :].rearrange("p (k n) -> p k n", k=KT), scalar=self.scale,
                                 in1=hi.bitcast(F32) if hi.dtype == F32R else hi,
                                 op0=ALU.mult, op1=ALU.subtract).then_inc(self.lo_done.sem, 1)


KB = 1024
MAT = KT * FP * 4
XN, XT_HI, XT_LO, GATE, PROD, Q, INNER_HI, INNER_LO, RAW, SPARE = (
    n * KB for n in (0, 4, 12, 20, 24, 28, 61, 83, 105, 171))
ARENA = SPARE + 16 * KB
AX_HI, AX_LO = RAW, RAW + MAT
AHEAD = Q + 34 * KB
UP_AHEAD = 2
GATE_AHEAD = FT - (NT - HEADSTART)


class FeedForward:

    def __init__(self, ctx, nc, tag, first, x, out_scale, ident, ones, q, place, banks, after=None):
        sb = lambda n, s, d=F32: ctx.enter_context(nc.sbuf_tensor(f"{n}_{tag}", s, d))
        sem = lambda n: ctx.enter_context(nc.semaphore(f"{n}_{tag}"))
        sig = lambda n, per=2: Signal(ctx, nc, f"{n}_{tag}", per, credit=True)
        self.first, self.x, self.out_scale, self.ones, self.after = first, x, out_scale, ones, after
        self.x_hi = place(f"xT_hi_{tag}", [P, KT, TOK], F16, XT_HI)
        self.x_lo = place(f"xT_lo_{tag}", [P, KT, TOK], F16, XT_LO)
        self.q = q
        self.inner_hi = place(f"inner_hi_{tag}", [P, FT, TOK], F16, INNER_HI)
        self.inner_lo = place(f"inner_lo_{tag}", [P, FT, TOK], F16, INNER_LO)
        self.gate = place(f"gate_{tag}", [P, 2, HALF], F32, GATE)
        self.prod = place(f"prod_{tag}", [P, 2, HALF], F32, PROD)
        self.gate_bank, self.up_bank, self.down_bank = banks["g"], banks["u"], banks["d"]
        xn = [place(f"xn{n}_{tag}", [P, HID], F32, at)[:, :]
              for n, at in enumerate((XN, XN + 2 * KB, PROD, PROD + 2 * KB))]
        self.norm = Norm(ctx, nc, tag, x, ident, self.x_hi, self.x_lo, X_SCALE, xn, banks["t"] + banks["u"])
        self.gate_ready, self.up_ready = sig("gate_ready"), sig("up_ready")
        self.gate_copied, self.prod_ready = sig("gate_copied"), sig("prod_ready")
        self.hi_done, self.lo_done = sig("inner_hi_done"), sig("inner_lo_done")
        self.down_ready, self.x_done = sig("down_ready"), sig("x_done")
        if first:
            self.raw = [place(f"raw{m}", [P, KT * FP], F32, RAW + m * MAT) for m in range(3)]
            self.sums, self.total = sb("sums", [P, 3, KT]), sb("total", [P, 3])
            self.above, self.below, self.mean = sb("above", [P, 3]), sb("below", [P, 3]), sb("mean", [P, 4])
            self.summed = [sem(f"summed{m}") for m in range(3)]
            self.neg = [sig(f"neg{m}_done") for m in range(3)]
            self.q_done = [sig(f"q{m}_done") for m in range(3)]
            self.sum_bcast, self.total_done, self.thresh, self.mean_done = map(
                sem, ("sum_bcast", "total_done", "thresh", "mean_done"))

    @staticmethod
    def flat(a):
        return a[:, :, :].rearrange("p a b -> p (a b)")


    def sum_magnitudes(self, act, m, c, loaded):
        act.wait_ge(loaded, 16)
        part = ds(c * FP, FP)
        act.activation(self.flat(self.q[m])[:, part], self.raw[m][:, part], ACT.Abs,
                       accum_out=self.sums[:, m, ds(c, 1)]).then_inc(self.summed[m], 1)

    def broadcast_sums(self, pe, m):
        pe.wait_ge(self.summed[m], KT)
        if m == 2:
            pe.wait_ge(self.total_done, 1)
        pe.matmul(self.down_bank[m % 2][:, 0:KT], self.ones[:, :], self.sums[:, m, :], start=True,
                  stop=True).then_inc(self.sum_bcast, 1)

    def thresholds(self, dve, m):
        n_w = FF * HID
        dve.wait_ge(self.sum_bcast, m + 1)
        dve.reduce_sum(self.total[:, m:m + 1], self.down_bank[m % 2][:, 0:KT], AX).then_inc(self.total_done, 1)
        dve.wait_ge(self.total_done, m + 1)
        total = self.total[:, m:m + 1]
        dve.tensor_scalar(self.above[:, m:m + 1], total, 0.5 / n_w, 0.5 * EPS, ALU.mult, ALU.add).then_inc(self.thresh, 1)
        dve.tensor_scalar(self.below[:, m:m + 1], total, -0.5 / n_w, -0.5 * EPS, ALU.mult,
                          ALU.add).then_inc(self.thresh, 1)
        dve.tensor_scalar(self.mean[:, m:m + 1], total, 1.0 / n_w, None, ALU.mult).then_inc(self.mean_done, 1)
        dve.wait_ge(self.thresh, 2 * (m + 1))

    def _part(self, a, m, i):
        return a[:, :, ds(i * P, P)] if m < 2 else a[:, ds(i, 1), :]

    def _raw(self, m):
        return self.raw[m][:, :].rearrange("p (a b) -> p a b", a=KT if m < 2 else FT)

    def is_below(self, dve, m, i):
        dve.tensor_scalar(self._part(self.q[m], m, i), self._part(self._raw(m), m, i), self.below[:, m:m + 1], None,
                          ALU.is_lt).then_inc(self.neg[m].sem, 1)

    def is_above(self, dve, m, i):
        dve.wait_ge(self.neg[m].sem, self.neg[m].now(0, i + 1))
        part = self._part(self.q[m], m, i)
        dve.scalar_tensor_tensor(out=part, in0=self._part(self._raw(m), m, i), scalar=self.above[:, m:m + 1], in1=part,
                                 op0=ALU.is_gt, op1=ALU.subtract).then_inc(self.q_done[m].sem, 1)

    def scales(self, dve):
        dve.wait_ge(self.mean_done, 3)
        dve.tensor_scalar(self.mean[:, 3:4], self.mean[:, 0:1], self.mean[:, 1:2], self.mean[:, 2:3],
                          ALU.mult, ALU.mult).then_inc(self.mean_done, 1)
        dve.wait_ge(self.mean_done, 4)
        dve.tensor_scalar(self.out_scale[:, :], self.mean[:, 3:4], 0.5 / INNER, None, ALU.mult).then_inc(self.mean_done, 1)
        dve.wait_ge(self.mean_done, 5)


    @staticmethod
    def pairs(eng, s, body, single):
        count = NT - HEADSTART if s == 0 else FT // 2
        with eng.Fori(0, count) as p:
            body(2 * p, s * FT + 2 * p, (s * FT % 2, (s * FT + 1) % 2), p)
        for i in range(2 * count, FT):
            single(i, s * FT + i, (s * FT + i) % 2)

    def inner_tensor(self, pe, weights_ready):
        norm = self.norm
        for t in range(HEADSTART):
            norm.transpose(pe, t, t, 0)
        if self.first:
            self.broadcast_sums(pe, 0)

        def product(m, s, i, n, slot, quarter=None):
            cols = slice(0, HALF) if quarter is None else slice(quarter * HALF // 2, (quarter + 1) * HALF // 2)
            bank, ready, freed = ((self.gate_bank, self.gate_ready, self.gate_copied),
                                  (self.up_bank, self.up_ready, self.prod_ready))[m]
            if s == 0:
                weights_ready(pe, m, i)
            pe.wait_ge(freed.sem, freed.last(0, n + 1))
            for k in range(KT):
                for part, xs in enumerate((self.x_hi, self.x_lo)):
                    last = pe.matmul(bank[slot][:, cols], self.q[m][:, k, ds(i * P, P)],
                                     xs[:, k, s * HALF + cols.start:s * HALF + cols.stop],
                                     start=k + part == 0, stop=k == KT - 1 and part == 1)
            if quarter != 0:
                last.then_inc(ready.sem, 1)

        for quarter in range(2):
            pe.wait_ge(norm.lo_done.sem, norm.lo_done.now(0, (quarter + 1) * HEADSTART // 2))
            product(0, 0, 0, 0, 0, quarter)
            if self.first and quarter == 1:
                self.broadcast_sums(pe, 1)
            product(0, 0, 1, 1, 1, quarter)

        def two(i, n, slots, p):
            for j in range(2):
                product(1, 0, i + j, n + j, slots[j])
                product(0, 0, i + j + 2, n + j + 2, slots[j])
            norm.transpose(pe, p + HEADSTART, 0, 1)

        def one(i, n, slot):
            product(1, 0, i, n, slot)
            if i + 2 < FT:
                product(0, 0, i + 2, n + 2, slot)

        self.pairs(pe, 0, two, one)
        if self.first:
            self.broadcast_sums(pe, 2)
        pe.wait_ge(norm.lo_done.sem, norm.lo_done.now(0, NT))

        def tile(i, n, slot):
            product(0, 1, i, n, slot)
            product(1, 1, i, n, slot)

        self.pairs(pe, 1, lambda i, n, slots, p: (tile(i, n, slots[0]), tile(i + 1, n + 1, slots[1])), tile)

    def inner_scalar(self, act, down_loaded):
        norm = self.norm
        for s in range(2):
            def copy_gate(n, slot):
                act.wait_ge(self.gate_ready.sem, self.gate_ready.now(0, n + 1))
                act.wait_ge(self.prod_ready.sem, self.prod_ready.last(0, n + 1))
                act.activation(self.gate[:, slot, :], self.gate_bank[slot][:, :], ACT.Copy,
                               scale=INNER / X_SCALE ** 2).then_inc(self.gate_copied.sem, 1)

            def hi(i, n, slot):
                act.wait_ge(self.prod_ready.sem, self.prod_ready.now(0, n + 1))
                act.activation(self.inner_hi[:, ds(i, 1), s * HALF:(s + 1) * HALF].rearrange("p a n -> p (a n)"),
                               self.prod[:, slot, :], ACT.Copy).then_inc(self.hi_done.sem, 1)

            def two(i, n, slots, p):
                copy_gate(n, slots[0])
                copy_gate(n + 1, slots[1])
                hi(i, n, slots[0])
                if s == 0 and self.first:
                    self.sum_magnitudes(act, 2, p, down_loaded)
                hi(i + 1, n + 1, slots[1])
                if s == 0:
                    norm.hi(act, p + HEADSTART, 0)

            def one(i, n, slot):
                copy_gate(n, slot)
                hi(i, n, slot)

            self.pairs(act, s, two, one)

    def multiply(self, dve, n, slot):
        dve.wait_ge(self.gate_copied.sem, self.gate_copied.now(0, n + 1))
        dve.wait_ge(self.up_ready.sem, self.up_ready.now(0, n + 1))
        dve.wait_ge(self.hi_done.sem, self.hi_done.last(0, n + 1))
        dve.wait_ge(self.lo_done.sem, self.lo_done.last(0, n + 1))
        dve.tensor_tensor(self.prod[:, slot, :], self.up_bank[slot][:, :], self.gate[:, slot, :],
                          ALU.mult).then_inc(self.prod_ready.sem, 1)

    def inner_vector(self, dve):
        norm = self.norm

        def ternary(m, i):
            self.is_below(dve, m, i)
            self.is_above(dve, m, i)

        for i in range(FT):
            t = HEADSTART + i // 2
            if i % 2 == 0 and t < NT:
                norm.stats(dve, t)
            self.multiply(dve, i, i % 2)
            if self.first and i + UP_AHEAD < FT:
                ternary(1, i + UP_AHEAD)
            if i % 2 == 0 and HEADSTART < t <= NT:
                norm.lo(dve, t - 1, 0)
            if i % 2 == 0 and t < NT:
                norm.normalize(dve, t, 0, 1)
            if i % 2 == 1 and t < NT and self.first:
                ternary(0, GATE_AHEAD + i // 2)

        if self.first:
            self.thresholds(dve, 2)
            self.scales(dve)

        def tile(i, n, slot):
            if self.first:
                ternary(2, i)
            self.multiply(dve, n, slot)

        self.pairs(dve, 1, lambda i, n, slots, p: (tile(i, n, slots[0]), tile(i + 1, n + 1, slots[1])), tile)

    def inner_pool(self, pool):
        for s in range(2):
            def lo(i, n, slot):
                pool.wait_ge(self.hi_done.sem, self.hi_done.now(0, n + 1))
                part = (slice(None), ds(i, 1), slice(s * HALF, (s + 1) * HALF))
                pool.tensor_tensor(self.inner_lo[part].rearrange("p a n -> p (a n)"), self.prod[:, slot, :],
                                   self.inner_hi[part].rearrange("p a n -> p (a n)"),
                                   ALU.subtract).then_inc(self.lo_done.sem, 1)

            def two(i, n, slots, p):
                if s == 0:
                    self.norm.rsqrt(pool, p + HEADSTART)
                lo(i, n, slots[0])
                lo(i + 1, n + 1, slots[1])

            self.pairs(pool, s, two, lo)


    @staticmethod
    def tiles(eng, step):
        step(0, 0)
        with eng.Fori(0, NT // 2 - 1) as p:
            step(2 * p + 1, 1)
            step(2 * p + 2, 0)
        step(NT - 1, 1)

    def down_tensor(self, pe):
        def step(t, slot):
            pe.wait_ge(self.x_done.sem, self.x_done.last(0, t + 1))
            for f in range(FT):
                if isinstance(t, int) and t == 0 and f in (0, FT - 1):
                    ready = 2 * FT if f else 2 * FT - 1
                    pe.wait_ge(self.hi_done.sem, self.hi_done.now(0, ready))
                    pe.wait_ge(self.lo_done.sem, self.lo_done.now(0, ready))
                    if self.first:
                        pe.wait_ge(self.q_done[2].sem, self.q_done[2].now(0, ready - FT))
                for part, inner in enumerate((self.inner_hi, self.inner_lo)):
                    last = pe.matmul(self.down_bank[slot][:, :], inner[:, f, ds(t * P, P)], self.q[2][:, f, :],
                                     start=f + part == 0, stop=f == FT - 1 and part == 1)
            last.then_inc(self.down_ready.sem, 1)
            if self.after and not (isinstance(t, int) and t == 0):
                self.after.transpose(pe, t - 1, 1 - slot, 2)

        self.tiles(pe, step)

    def down_scalar(self, act):
        def step(t, slot):
            if not (isinstance(t, int) and t == 0):
                self.after.hi(act, t - 1, 1 - slot)

        self.tiles(act, step)

    def down_pool(self, pool):
        for t in range(NT):
            self.after.rsqrt(pool, t)

    def down_vector(self, dve):
        def step(t, slot):
            dve.wait_ge(self.down_ready.sem, self.down_ready.now(0, t + 1))
            xt = self.x[:, ds(t, 1), :].rearrange("p a n -> p (a n)")
            dve.scalar_tensor_tensor(out=xt, in0=self.down_bank[slot][:, :], scalar=self.out_scale[:, 0:1], in1=xt,
                                     op0=ALU.mult, op1=ALU.add).then_inc(self.x_done.sem, 1)
            if self.after:
                dve.wait_ge(self.x_done.sem, self.x_done.now(0, t + 1))
                self.after.stats(dve, t)
                if not (isinstance(t, int) and t == 0):
                    self.after.lo(dve, t - 1, 1 - slot)
                self.after.normalize(dve, t, slot, 2)

        if self.after:
            for t in range(NT):
                step(t, t % 2)
        else:
            self.tiles(dve, step)

    def head_vector(self, dve):
        norm = self.norm
        norm.stats(dve, 0)
        norm.stats(dve, 1)
        for t in range(HEADSTART):
            norm.normalize(dve, t, t, 0)
            if t + 2 < HEADSTART:
                norm.stats(dve, t + 2)
            if t >= 2:
                norm.lo(dve, t - 2, t - 2)
        for t in range(HEADSTART - 2, HEADSTART):
            norm.lo(dve, t, t)


def ffn_banks(ctx, nc, tag):
    return {n: [ctx.enter_context(nc.psum_tensor(f"{n}{j}_{tag}", [P, HALF], F32)) for j in range(2)] for n in "tgud"}


def first_half(nc, place, x, x_in, x_hi, x_lo, stats, out_scale, ident, ones, q, weights, ternary, squares_in,
               w_v_in, w_in_in, dt_bias_in, a_log_in, v_dram, g_dram, first_loads, v_stored):
    with ExitStack() as ctx:
        sb = lambda n, s, d=F32: ctx.enter_context(nc.sbuf_tensor(n, s, d))
        sem = lambda n: ctx.enter_context(nc.semaphore(n))
        banks = ffn_banks(ctx, nc, "ffn1")
        after_xn = [place(f"xn{n}_attn", [P, HID], F32, XT_LO + n * 2 * KB)[:, :] for n in range(2)]
        after = Norm(ctx, nc, "attn", x, ident, x_hi, x_lo, 1.0, after_xn, banks["t"])
        ffn = FeedForward(ctx, nc, "ffn1", True, x, out_scale, ident, ones, q, place, banks, after)
        small = RAW + 2 * MAT
        wv_raw = place("wv_raw", [P, KT, KVH * D], F32, SPARE)
        win_raw = place("win_raw", [P, KT, H], F32, small + 16 * KB)
        win_hi = place("win_hi", [P, KT, P], F32R, small + 17 * KB)
        win_lo = place("win_lo", [P, KT, P], F32R, small + 19 * KB)
        wv_hi = place("wv_hi", [P, KT, KVH * D], F32R, Q)
        wv_lo = place("wv_lo", [P, KT, KVH * D], F32R, small)
        v = place("v_tiles", [P, 4, HALF], F32, GATE)
        pre_t, g_t = place("pre_t", [H, TOK], F32, AHEAD), place("g_t", [H, TOK], F32, AHEAD + 4 * KB)
        names = "pre mag expo one_plus ln_u back rest recip corr pos a_exp g cum".split()
        pre, mag, e, u, ln_u, d, rest, ru, corr, pos, a, g, G = (
            place(n, [P, NT * H], F32, INNER_LO + j * KB) for j, n in enumerate(names))
        dt_bias = sb("dt_bias", [H, 1])
        tri = place("tri", [P, P], F32, small + 16 * KB + KB // 2)
        a_log = place("a_log", [P, NT * H], F32, small + 21 * KB)
        v_bank, b = banks["g"], banks["u"] + banks["d"]

        x_loaded = [sem(f"x_loaded{s}") for s in range(2)]
        const_loaded, ones_ready = sem("const_loaded"), sem("ones_ready")
        w_loaded = [[sem(f"w{m}_loaded{c}") for c in range(KT)] for m in range(2)] + [[sem("w2_loaded")]]
        q_stored = [sem(f"q{m}_stored") for m in range(3)]
        loaded = {n: sem(f"{n}_loaded") for n in ("tri", "wv", "win", "bias", "alog")}
        cleared, split_hi, split_lo, split_lo_dve = map(sem, ("win_cleared", "split_hi", "split_lo", "split_lo_dve"))
        pre_ready, pre_copied, nat_ready, step, act_step = map(
            sem, ("pre_ready", "pre_copied", "nat_ready", "dt_step", "dt_act_step"))
        cum_ready, cum_copied, gt_ready, gt_copied, g_stored = map(
            sem, ("cum_ready", "cum_copied", "gt_ready", "gt_copied", "g_stored"))
        v_ready, v_copied = sem("v_ready"), sem("v_copied")
        dt_out = stats[:, 0:NT, :].rearrange("p t h -> p (t h)")
        NV = 2 * NT
        block = ctx.enter_context(nc.Block())

        @block.sync
        def _(sp):
            half = NT // 2
            sp.dma_start(x[:, 0:half, :], x_in[:, 0:half, :]).then_inc(x_loaded[0], 16)
            sp.dma_start(ident[:, :], squares_in[:, 0, :]).then_inc(const_loaded, 16)
            for m in range(2):
                for c in range(KT):
                    part = slice(c * FP, (c + 1) * FP)
                    sp.dma_start(ffn.raw[m][:, part], weights[m][:, part]).then_inc(w_loaded[m][c], 16)
            sp.dma_start(x[:, half:NT, :], x_in[:, half:NT, :]).then_inc(x_loaded[1], 16)
            sp.dma_start(ffn.raw[2][:, :], weights[2]).then_inc(w_loaded[2][0], 16)
            sp.dma_start(wv_raw[:, :, :], w_v_in).then_inc(loaded["wv"], 16)
            sp.dma_start(dt_bias[:, :], dt_bias_in).then_inc(loaded["bias"], 16)
            for m in range(3):
                sp.wait_ge(ffn.q_done[m].sem, ffn.q_done[m].now(0, FT))
                sp.dma_start(ternary[m], ffn.flat(ffn.q[m])).then_inc(q_stored[m], 16)
            sp.dma_start(win_raw[:, :, :], w_in_in).then_inc(loaded["win"], 16)
            sp.dma_start(tri[:, :], squares_in[:, 1, :]).then_inc(loaded["tri"], 16)
            sp.dma_start(a_log[:, :], a_log_in.partition_broadcast(P)).then_inc(loaded["alog"], 16)
            sp.wait_ge(ffn.down_ready.sem, ffn.down_ready.now(0, NT))
            sp.wait_ge(q_stored[2], 16)
            first_loads(sp)
            for n in range(NV):
                t, s = n // 2, n % 2
                if n == 10:
                    sp.wait_ge(gt_copied, 2)
                    sp.dma_start(g_dram, g_t[:, :]).then_inc(g_stored, 16)
                sp.wait_ge(v_copied, n + 1)
                sp.dma_start(v_dram[4 * s:4 * s + 4, :, t, :].rearrange("g p e -> p g e"),
                             v[:, n % 4, :].rearrange("p (g e) -> p g e", g=4)).then_inc(v_stored[n % 4], 16)
            sp.wait_ge(g_stored, 16)
            sp.wait_ge(q_stored[2], 16)

        @block.gpsimd
        def _(pool):
            ffn.norm.start_pool(pool)
            after.start_pool(pool)
            ffn.lo_done.start(pool)
            for t in range(HEADSTART):
                ffn.norm.rsqrt(pool, t)
            ffn.inner_pool(pool)
            pool.wait_ge(ffn.q_done[2].sem, ffn.q_done[2].now(0, FT))
            for m in (win_hi, win_lo):
                pool.memset(m[:, :, :].bitcast(F32), 0.0).then_inc(cleared, 1)
            pool.wait_ge(cleared, 2)
            pool.wait_ge(split_hi, 1)
            pool.tensor_tensor(wv_lo[:, 0, :], wv_raw[:, 0, :], wv_hi[:, 0, :].bitcast(F32),
                               ALU.subtract).then_inc(split_lo, 1)
            pool.wait_ge(split_hi, KT + 1)
            pool.tensor_tensor(win_lo[:, :, 0:H], win_raw[:, :, :], win_hi[:, :, 0:H].bitcast(F32),
                               ALU.subtract).then_inc(split_lo, 1)
            ffn.down_pool(pool)

        @block.scalar
        def _(act):
            for sg in (ffn.gate_copied, ffn.hi_done, ffn.norm.hi_done, after.hi_done):
                sg.start(act)
            for t in range(HEADSTART):
                ffn.sum_magnitudes(act, 0, t, w_loaded[0][t])
                ffn.norm.hi(act, t, t)
            for c in range(KT):
                ffn.sum_magnitudes(act, 1, c, w_loaded[1][c])
            ffn.inner_scalar(act, w_loaded[2][0])
            act.wait_ge(loaded["wv"], 16)
            for m in range(2):
                act.wait_ge(q_stored[m], 16)
            act.wait_ge(ffn.up_ready.sem, ffn.up_ready.now(0, 2 * FT))
            for k in range(KT):
                act.activation(wv_hi[:, k, :], wv_raw[:, k, :], ACT.Copy).then_inc(split_hi, 1)
            act.wait_ge(loaded["win"], 16)
            act.wait_ge(cleared, 2)
            act.activation(win_hi[:, :, 0:H], win_raw[:, :, :], ACT.Copy).then_inc(split_hi, 1)
            ffn.down_scalar(act)

            def v_copy(n):
                act.wait_ge(v_ready, n + 1)
                if n >= 4:
                    act.wait_ge(v_stored[n % 4], 16 * (n // 4))
                act.activation(v[:, n % 4, :], v_bank[n % 2][:, :], ACT.Copy).then_inc(v_copied, 1)

            v_copy(0)
            v_copy(1)
            after.hi(act, NT - 1, 1)
            v_copy(2)
            act.wait_ge(loaded["bias"], 16)
            for s in range(2):
                act.wait_ge(pre_ready, s + 1)
                act.activation(pre_t[:, s * HALF:(s + 1) * HALF], b[s][0:H, :], ACT.Identity,
                               bias=dt_bias[:, 0:1]).then_inc(pre_copied, 1)
            v_copy(3)
            act.wait_ge(step, 1)
            act.activation(mag[:, :], pre[:, :], ACT.Abs).then_inc(act_step, 1)
            act.wait_ge(act_step, 1)
            act.activation(e[:, :], mag[:, :], ACT.Exp, scale=-1.0).then_inc(act_step, 1)
            act.wait_ge(step, 2)
            act.activation(ln_u[:, :], u[:, :], ACT.Ln).then_inc(act_step, 1)
            act.wait_ge(loaded["alog"], 16)
            act.activation(a[:, :], a_log[:, :], ACT.Exp).then_inc(act_step, 1)
            for n in range(4, 8):
                v_copy(n)
            act.wait_ge(cum_ready, 1)
            act.activation(G[:, :], b[0][:, 0:NT * H], ACT.Copy).then_inc(cum_copied, 1)
            v_copy(8)
            for s in range(2):
                act.wait_ge(gt_ready, s + 1)
                act.activation(g_t[:, s * HALF:(s + 1) * HALF], b[2 + s][0:H, :], ACT.Copy).then_inc(gt_copied, 1)
            for n in range(9, NV):
                v_copy(n)

        @block.vector
        def _(dve):
            for sg in (ffn.prod_ready, ffn.x_done, *ffn.neg, *ffn.q_done):
                sg.start(dve)
            ffn.norm.start_vector(dve)
            after.start_vector(dve)
            dve.memset(ones[:, :], 1.0).then_inc(ones_ready, 1)
            dve.wait_ge(x_loaded[0], 16)
            ffn.head_vector(dve)
            ffn.thresholds(dve, 0)

            def ternary(m, tiles):
                for i in tiles:
                    ffn.is_below(dve, m, i)
                for i in tiles:
                    ffn.is_above(dve, m, i)

            ternary(0, (0,))
            ternary(0, (1, 2))
            ternary(0, (3, 4))
            ffn.thresholds(dve, 1)
            ternary(1, (0,))
            ternary(0, range(5, GATE_AHEAD))
            ternary(1, range(1, UP_AHEAD))
            dve.wait_ge(x_loaded[1], 16)
            ffn.inner_vector(dve)
            for k in range(1, KT):
                dve.wait_ge(split_hi, k + 1)
                dve.tensor_tensor(wv_lo[:, k, :], wv_raw[:, k, :], wv_hi[:, k, :].bitcast(F32),
                                  ALU.subtract).then_inc(split_lo_dve, 1)
            ffn.down_vector(dve)
            after.lo(dve, NT - 1, 1)
            done = [0]

            def own(ins):
                done[0] += 1
                ins.then_inc(step, 1)
                dve.wait_ge(step, done[0])

            dve.wait_ge(nat_ready, 1)
            own(dve.tensor_copy(pre[:, :], b[2][:, 0:NT * H]))
            dve.wait_ge(act_step, 2)
            own(dve.tensor_scalar(u[:, :], e[:, :], 1.0, None, ALU.add))
            own(dve.tensor_scalar(d[:, :], u[:, :], -1.0, None, ALU.add))
            own(dve.tensor_tensor(rest[:, :], e[:, :], d[:, :], ALU.subtract))
            own(dve.reciprocal(ru[:, :], u[:, :]))
            own(dve.tensor_tensor(corr[:, :], rest[:, :], ru[:, :], ALU.mult))
            own(dve.scalar_tensor_tensor(out=pos[:, :], in0=pre[:, :], scalar=0.0, in1=corr[:, :],
                                         op0=ALU.max, op1=ALU.add))
            dve.wait_ge(act_step, 4)
            own(dve.tensor_tensor(dt_out, pos[:, :], ln_u[:, :], ALU.add))
            own(dve.scalar_tensor_tensor(out=g[:, :], in0=dt_out, scalar=-1.0, in1=a[:, :],
                                         op0=ALU.mult, op1=ALU.mult))
            dve.wait_ge(cum_copied, 1)
            own(dve.tensor_scalar(stats[:, NT:2 * NT, :].rearrange("p t h -> p (t h)"), G[:, :], -1.0, None, ALU.mult))
            dve.wait_ge(cum_ready, 2)
            first_chunks = lambda m: m.rearrange("p (b c h) -> p b c h", b=B, c=2)[:, :, 0, :]
            own(dve.tensor_tensor(stats[:, 2 * NT:2 * NT + B, :], first_chunks(b[1][:, 0:NT * H]),
                                  first_chunks(G[:, :]), ALU.subtract))

        @block.tensor
        def _(pe):
            for sg in (ffn.gate_ready, ffn.up_ready, ffn.down_ready, ffn.norm.t_ready, after.t_ready):
                sg.start(pe)
            pe.wait_ge(const_loaded, 16)
            pe.wait_ge(ones_ready, 1)
            ffn.inner_tensor(pe, lambda eng, m, i: eng.wait_ge(ffn.q_done[m].sem, ffn.q_done[m].now(0, i + 1)))
            ffn.down_tensor(pe)

            def project_v(n):
                t, s = n // 2, n % 2
                if n >= 2:
                    pe.wait_ge(v_copied, n - 1)
                for k in range(KT):
                    for m, (xs, w) in enumerate(((x_hi, wv_hi), (x_lo, wv_hi), (x_hi, wv_lo))):
                        last = pe.matmul(v_bank[n % 2][:, :], xs[:, k, t * P:(t + 1) * P],
                                         w[:, k, s * HALF:(s + 1) * HALF], start=k + m == 0,
                                         stop=k == KT - 1 and m == 2)
                last.then_inc(v_ready, 1)

            pe.wait_ge(split_hi, 1 + KT)
            pe.wait_ge(split_lo, 2)
            pe.wait_ge(split_lo_dve, KT - 1)
            pe.wait_ge(after.lo_done.sem, after.lo_done.now(0, 1))
            project_v(0)
            project_v(1)
            after.transpose(pe, NT - 1, 1, 2)
            project_v(2)
            pe.wait_ge(after.lo_done.sem, after.lo_done.now(0, NT))
            pe.wait_ge(ffn.x_done.sem, ffn.x_done.now(0, NT))
            for s in range(2):
                cols = slice(s * HALF, (s + 1) * HALF)
                for k in range(KT):
                    for n, (w, xs) in enumerate(((win_hi, x_hi), (win_hi, x_lo), (win_lo, x_hi))):
                        last = pe.matmul(b[s][:, :], w[:, k, :], xs[:, k, cols], start=k + n == 0,
                                         stop=k == KT - 1 and n == 2)
                last.then_inc(pre_ready, 1)
            project_v(3)
            pe.wait_ge(pre_copied, 2)
            for t in range(NT):
                last = pe.transpose(b[2][:, t * H:(t + 1) * H], pre_t[:, t * P:(t + 1) * P], ident[0:H, 0:H])
            last.then_inc(nat_ready, 1)
            for n in range(4, 8):
                project_v(n)
            pe.wait_ge(loaded["tri"], 16)
            pe.wait_ge(step, 9)
            pe.matmul(b[0][:, 0:NT * H], tri[:, :], g[:, :], start=True, stop=True).then_inc(cum_ready, 1)
            pe.matmul(b[1][:, 0:NT * H], ones[:, :], g[:, :], start=True, stop=True).then_inc(cum_ready, 1)
            project_v(8)
            pe.wait_ge(cum_copied, 1)
            for s in range(2):
                for t in range(4):
                    tt = 4 * s + t
                    last = pe.transpose(b[2 + s][0:H, t * P:(t + 1) * P], G[:, tt * H:(tt + 1) * H], ident[:, :])
                last.then_inc(gt_ready, 1)
            for n in range(9, NV):
                project_v(n)


def second_ffn(nc, place, x, out_scale, ident, ones, q, q_loaded, out):
    with ExitStack() as ctx:
        sem = lambda n: ctx.enter_context(nc.semaphore(n))
        ffn = FeedForward(ctx, nc, "ffn2", False, x, out_scale, ident, ones, q, place, ffn_banks(ctx, nc, "ffn2"))
        stored = sem("out_stored")
        block = ctx.enter_context(nc.Block())

        @block.sync
        def _(sp):
            for t in range(NT):
                sp.wait_ge(ffn.x_done.sem, ffn.x_done.now(0, t + 1))
                sp.dma_start(out[:, t, :], x[:, t, :]).then_inc(stored, 16)
            sp.wait_ge(stored, 16 * NT)

        @block.gpsimd
        def _(pool):
            ffn.lo_done.start(pool)
            ffn.norm.start_pool(pool)
            for t in range(HEADSTART):
                ffn.norm.rsqrt(pool, t)
            ffn.inner_pool(pool)

        @block.scalar
        def _(act):
            for sg in (ffn.gate_copied, ffn.hi_done, ffn.norm.hi_done):
                sg.start(act)
            for t in range(HEADSTART):
                ffn.norm.hi(act, t, t)
            ffn.inner_scalar(act, None)

        @block.vector
        def _(dve):
            for sg in (ffn.prod_ready, ffn.x_done):
                sg.start(dve)
            ffn.norm.start_vector(dve)
            ffn.head_vector(dve)
            ffn.inner_vector(dve)
            ffn.down_vector(dve)

        @block.tensor
        def _(pe):
            for sg in (ffn.gate_ready, ffn.up_ready, ffn.down_ready, ffn.norm.t_ready):
                sg.start(pe)
            pe.wait_ge(q_loaded[0], 16)
            pe.wait_ge(q_loaded[1], 16)
            ffn.inner_tensor(pe, lambda eng, m, i: None)
            pe.wait_ge(q_loaded[2], 16)
            ffn.down_tensor(pe)




def steps(text):
    return [(s[0], int(s[1:])) for s in text.split()]


ORDER = {
    "tensor": steps(
        "R0 R1 R2 R3 G0 R4 R5 G1 R6 R7 S0 S1 G2 Y0 S2 S3 G3 S4 S5 Y1 T0 R8 R9 Y2 T1 G4 G5 Y3 S6 S7 T2 O0 S8 "
        "Y4 S9 O1 S10 T3 S11 Y5 G6 G7 Y6 T4 O2 O3 Y7 T5 O4 T6 O5 T7 O6 O7"),
    "scalar": steps(
        "W0 W1 W2 R0 R1 K0 R2 R3 K1 W3 G0 K2 K3 R4 R5 E0 E1 K4 K5 G1 R6 R7 E2 E3 Y0 E4 G2 G3 K6 K7 E5 Y1 E6 "
        "T0 R8 R9 Y2 E7 G4 K8 K9 G5 T1 Y3 E8 E9 T2 Y4 E10 E11 Y5 T3 G6 G7 Y6 T4 Y7 T5 T6 T7"),
    "vector": steps(
        "H0 W1 C0 C1 A0 A1 L0 C2 L1 C3 A2 A3 L2 L3 C4 C5 A4 A5 L4 L5 G0 G1 C6 P0 P1 C7 A6 A7 P2 P3 Y0 P4 L6 "
        "L7 G2 G3 Y1 T0 C8 P5 C9 A8 A9 Y2 L8 L9 G4 T1 P6 P7 Y3 G5 P8 P9 T2 Y4 X0 X1 T3 Y5 G6 G7 P10 P11 Y6 T4 "
        "X2 X3 T5 Y7 T6 X4 X5 T7 X6 X7"),
    "gpsimd": steps(
        "W0 W2 R0 R1 R2 R3 M0 M1 M2 R4 R5 W3 R6 R7 Y0 M3 M4 M5 Y1 R8 R9 Y2 M6 Y3 Y4 M7 Y5 Y6 Y7"),
}
NR = 2 + 2 * REP
SHARED = [p for p in ORDER["tensor"] if p[0] in "GO"]
BLOCKS = ((0, 0), (0, 1), (1, 1))


class AttentionInputs:

    def __init__(self, ctx, nc, place, w_q, w_k, w_g, w_o, tables, gnorm):
        sem = lambda n: ctx.enter_context(nc.semaphore(n))
        self.w_q, self.w_k, self.w_g, self.w_o, self.table_in, self.gnorm_in = w_q, w_k, w_g, w_o, tables, gnorm
        self.tables = place("rotary_and_mask", [P, 3, HALF], F32, XN)
        self.gnorm = ctx.enter_context(nc.sbuf_tensor("gnorm", [P, 1], F32))
        self.raw_g = place("raw_g", [P, KT, HALF], F32, Q + 16 * KB)
        self.raw_qo = place("raw_qo", [P, KT, HALF], F32, Q + 24 * KB)
        self.raw_k = place("raw_k", [P, KT, D], F32, Q + 32 * KB)
        self.table_loaded = sem("table_loaded")
        self.k, self.g = Signal(ctx, nc, "load_k", 16), Signal(ctx, nc, "load_g", 16)
        self.qo = Signal(ctx, nc, "load_qo", 32)

    def load(self, sp, raw, w, g, sg):
        sp.dma_start(raw[:, :, :], w[ds(g, 1), :, :, :].rearrange("a p k n -> (a p) k n")).then_inc(sg.sem, 16)

    def first_loads(self, sp):
        self.load(sp, self.raw_k, self.w_k, 0, self.k)
        self.load(sp, self.raw_qo, self.w_q, 0, self.qo)
        self.load(sp, self.raw_g, self.w_g, 0, self.g)
        sp.dma_start(self.tables[:, :, :], self.table_in).then_inc(self.table_loaded, 16)
        sp.dma_start(self.gnorm[:, :], self.gnorm_in).then_inc(self.table_loaded, 16)


def attention(nc, place, x, ident, x_hi, x_lo, stats, ins, v_dram, g_dram, v_stored, q, ternary, q_loaded):
    with ExitStack() as ctx:
        sb = place.between(((XN + 6 * KB, GATE), (AHEAD, AX_HI), (AX_HI + 16 * KB, AX_LO), (AX_LO + 16 * KB, ARENA)))
        sem = lambda n: ctx.enter_context(nc.semaphore(n))
        sig = lambda n, per: Signal(ctx, nc, n, per, credit=True)
        bank = lambda n: ctx.enter_context(nc.psum_tensor(n, [P, HALF], F32))

        cos, sin, mask = (ins.tables[:, n, :] for n in range(3))
        gnorm, raw_k, raw_g, raw_qo, table_loaded = ins.gnorm, ins.raw_k, ins.raw_g, ins.raw_qo, ins.table_loaded
        prob = sb("prob", [P, 2, len(BLOCKS), REP, P])
        wk_hi = sb("wk_hi", [P, KT, D], F32R)
        w = {n: (sb(f"w{n}_hi", [P, KT, HALF], F32R), sb(f"w{n}_lo", [P, KT, HALF], F32R)) for n in "go"}
        w["q"] = (place("wq_hi", [P, KT, HALF], F32R, Q), place("wq_lo", [P, KT, HALF], F32R, Q + 8 * KB))
        raw = {"k": raw_k, "q": raw_qo, "g": raw_g, "o": raw_qo}
        k_hi, k_lo = sb("k_hi", [P, TOK], F32R), sb("k_lo", [P, TOK], F32R)
        w["k"] = (wk_hi, sb("wk_lo", [P, KT, D], F32R))
        junk = sb("squares", [P, REP, D], F16)
        v = sb("v", [P, NT, D])
        g_masked = sb("g_masked", [P, REP, P])
        q_hi, q_lo = sb("q_hi", [P, REP + 1, HALF], F32R), sb("q_lo", [P, REP + 1, HALF], F32R)
        rot_a, rot_b = sb("rot_cos", [P, 2, HALF]), sb("rot_sin", [P, 2, HALF])
        z = sb("z", [P, 4, REP, D])
        z_hi, z_lo = sb("z_t_hi", [P, 2, REP, P], F32R), sb("z_t_lo", [P, 2, REP, P], F32R)
        g_rows = place("g_rows", [P, 2, REP, L], F32, GATE)
        tiny = lambda n, s: ctx.enter_context(nc.sbuf_tensor(n, s, F32))
        eps4, power = tiny("eps4", [P, REP]), tiny("neg_half", [P, REP])
        sumsq, sum_eps, rinv = (tiny(n, [P, NT, REP]) for n in ("sumsq", "sum_eps", "rinv"))
        head = tiny("head_stats", [P, 2 * NT + B, REP])
        rot_bank, mul_bank, s_bank = [bank("r0"), bank("r1")], [bank("j0"), bank("j1")], [bank("s0"), bank("s1")]
        y_bank, z_bank = bank("y"), bank("zt")

        consts_ready = sem("attn_consts")
        ld_k, ld_g, ld_qo, ld_v = ins.k, ins.g, ins.qo, Signal(ctx, nc, "load_v", 16)
        ld_rows = [Signal(ctx, nc, f"load_rows{n}", 32) for n in range(2)]
        hi_done = sig("w_hi_done", 4)
        lo_done, q_lo_done = sig("w_lo_done", 3), sig("wq_lo_done", 1)
        rot_ready, cos_done, swap_done = sig("rot_ready", NR), sig("cos_done", NR), sig("swap_done", NR)
        sin_done, rot_done = sig("sin_done", NR), sig("rot_done", NR)
        qk_hi_done, qk_lo_done = sig("qk_hi_done", NR), sig("qk_lo_done", NR)
        mul_ready = sig("mul_ready", len(SHARED))
        tanh_done, silu_done, x_added = sig("tanh_done", NT), sig("silu_done", NT), sig("x_added", NT)
        mask_done, decay_done = sig("mask_done", 2 * B), sig("decay_done", 3 * B)
        score_ready, prob_done = sig("score_ready", 3 * B), sig("prob_done", 3 * B)
        y_ready, square_done, eps_done, rinv_done = (sig(n, NT) for n in ("y_ready", "square_done", "eps_done",
                                                                         "rinv_done"))
        z_done, zt_ready, zhi_done, zlo_done = (sig(n, NT) for n in ("z_done", "zt_ready", "zhi_done", "zlo_done"))
        head_copied = sig("head_copied", 1)

        def used(sg, g, n, ring):
            return sg.now(g, n - ring + 1) if n >= ring else sg.last(g, sg.per + n - ring + 1)

        def rotated(part, n):
            if n < 2:
                return (k_hi, k_lo)[part][:, n * HALF:(n + 1) * HALF]
            s, h = (n - 2) // REP, (n - 2) % REP
            return (q_hi, q_lo)[part][:, 1 - s + h, :]

        def mul_at(what, t):
            return SHARED.index((what, t))

        block = ctx.enter_context(nc.Block())

        @block.sync
        def _(sp):
            def this_pass(g):
                sp.wait_ge(q_lo_done.sem, q_lo_done.now(g, 1))
                ins.load(sp, raw_qo, ins.w_o, g, ld_qo)
                sp.wait_ge(y_ready.sem, y_ready.last(g, NT))
                sp.dma_start(v[:, :, :], v_dram[ds(g, 1), :, :, :].rearrange("a p k n -> (a p) k n")
                             ).then_inc(ld_v.sem, 16)
                for b in range(B):
                    sp.wait_ge(decay_done.sem, decay_done.now(g, 3 * (b - 1)) if b >= 2 else
                               decay_done.last(g, 3 * (B + b - 1)))
                    sp.dma_start(g_rows[:, b % 2, :, :],
                                 g_dram[ds(g * REP, REP), b * L:(b + 1) * L].partition_broadcast(P)
                                 ).then_inc(ld_rows[b % 2].sem, 16)

            for n in range(4):
                sp.wait_ge(v_stored[n], 16 * 2 * NT // 4)
            with sp.Fori(0, KVH - 1) as g:
                this_pass(g)
                sp.wait_ge(lo_done.sem, lo_done.now(g, 1))
                ins.load(sp, raw_k, ins.w_k, g + 1, ld_k)
                sp.wait_ge(lo_done.sem, lo_done.now(g, 3))
                ins.load(sp, raw_qo, ins.w_q, g + 1, ld_qo)
                ins.load(sp, raw_g, ins.w_g, g + 1, ld_g)
            this_pass(KVH - 1)
            sp.wait_ge(lo_done.sem, lo_done.now(KVH - 1, 3))
            sp.wait_ge(rot_ready.sem, rot_ready.now(KVH - 1, NR))
            for m in range(3):
                sp.dma_start(q[m][:, :, :].rearrange("p a b -> p (a b)"), ternary[m]).then_inc(q_loaded[m], 16)

        @block.gpsimd
        def _(pool):
            for sg in (lo_done, sin_done, mask_done, eps_done, rinv_done):
                sg.start(pool)
            pool.memset(eps4[:, :], 4 * EPS).then_inc(consts_ready, 1)
            pool.memset(power[:, :], -0.5).then_inc(consts_ready, 1)
            pool.wait_ge(consts_ready, 2)
            pool.wait_ge(table_loaded, 32)
            with pool.Fori(0, KVH) as g:

                def split_lo(n):
                    name = "kqgo"[n]
                    pool.wait_ge(hi_done.sem, hi_done.now(g, n + 1))
                    pool.tensor_tensor(w[name][1][:, :, :], raw[name][:, :, :], w[name][0][:, :, :].bitcast(F32),
                                       ALU.subtract).then_inc(lo_done.sem, 1)

                for what, n in ORDER["gpsimd"]:
                    if what == "W":
                        split_lo(n)
                    elif what == "R":
                        pool.wait_ge(swap_done.sem, swap_done.now(g, n + 1))
                        pool.tensor_tensor(rot_b[:, n % 2, :], rot_b[:, n % 2, :], sin,
                                           ALU.mult).then_inc(sin_done.sem, 1)
                    elif what == "M":
                        b, chunk = n // 2, n % 2
                        rows = g_rows[:, b % 2, :, chunk * P:(chunk + 1) * P]
                        causal = mask.rearrange("p (h i) -> p h i", h=REP)
                        pool.wait_ge(ld_rows[b % 2].sem, ld_rows[b % 2].now(g, 16 * (b // 2 + 1)))
                        if chunk:
                            pool.wait_ge(decay_done.sem, decay_done.now(g, 3 * b) if b else decay_done.last(g, 3 * B))
                            masked = g_masked[:, :, :]
                        else:
                            masked = rows
                        pool.tensor_tensor(masked, rows, causal, ALU.add).then_inc(mask_done.sem, 1)
                    elif what == "Y":
                        pool.wait_ge(square_done.sem, square_done.now(g, n + 1))
                        pool.tensor_tensor(sum_eps[:, n, :], sumsq[:, n, :], eps4[:, :], ALU.add).then_inc(eps_done.sem, 1)
                        pool.wait_ge(eps_done.sem, eps_done.now(g, n + 1))
                        pool.tensor_tensor(rinv[:, n, :], sum_eps[:, n, :], power[:, :], ALU.pow).then_inc(rinv_done.sem, 1)

        @block.scalar
        def _(act):
            for sg in (hi_done, swap_done, qk_hi_done, tanh_done, decay_done, square_done, zhi_done):
                sg.start(act)
            act.wait_ge(table_loaded, 32)
            with act.Fori(0, KVH) as g:

                def split_hi(n):
                    name = "kqgo"[n]
                    loaded, count = ((ld_k, 16), (ld_qo, 16), (ld_g, 16), (ld_qo, 32))[n]
                    act.wait_ge(loaded.sem, loaded.now(g, count))
                    user, k = ((rot_ready, 2), (rot_ready, NR), (mul_ready, mul_at("G", NT - 1) + 1),
                               (mul_ready, len(SHARED)))[n]
                    act.wait_ge(user.sem, user.last(g, k))
                    act.activation(w[name][0][:, :, :], raw[name][:, :, :], ACT.Copy).then_inc(hi_done.sem, 1)

                for what, n in ORDER["scalar"]:
                    if what == "W":
                        split_hi(n)
                    elif what == "R":
                        act.wait_ge(rot_ready.sem, rot_ready.now(g, n + 1))
                        act.wait_ge(rot_done.sem, used(rot_done, g, n, 2))
                        act.activation(rot_b[0:64, n % 2, :], rot_bank[n % 2][64:128, :], ACT.Copy)
                        act.activation(rot_b[64:128, n % 2, :], rot_bank[n % 2][0:64, :],
                                       ACT.Copy).then_inc(swap_done.sem, 1)
                    elif what == "K":
                        act.wait_ge(rot_done.sem, rot_done.now(g, n + 1))
                        if n == 0:
                            act.wait_ge(score_ready.sem, score_ready.last(g, 3 * B))
                        elif n == 2 + REP + 1:
                            act.wait_ge(score_ready.sem, score_ready.now(g, 3 * B // 2))
                        act.activation(rotated(0, n), rot_a[:, n % 2, :], ACT.Copy).then_inc(qk_hi_done.sem, 1)
                    elif what == "E":
                        b, m = n // 3, n % 3
                        if m == 0:
                            act.wait_ge(head_copied.sem, head_copied.now(g, 1))
                            act.wait_ge(y_ready.sem, used(y_ready, g, 2 * b + 1, 4))
                            act.wait_ge(mask_done.sem, mask_done.now(g, 2 * b + 1))
                        elif m == 2:
                            act.wait_ge(mask_done.sem, mask_done.now(g, 2 * b + 2))
                        for h in range(REP):
                            if m == 0:
                                rows, bias = g_rows[:, b % 2, h, 0:P], head[:, NT + 2 * b, h:h + 1]
                            elif m == 1:
                                rows, bias = g_rows[:, b % 2, h, P:L], head[:, 2 * NT + b, h:h + 1]
                            else:
                                rows, bias = g_masked[:, h, :], head[:, NT + 2 * b + 1, h:h + 1]
                            last = act.activation(prob[:, b % 2, m, h, :], rows, ACT.Exp, bias=bias)
                        last.then_inc(decay_done.sem, 1)
                    elif what == "G":
                        m = mul_at("G", n)
                        act.wait_ge(mul_ready.sem, mul_ready.now(g, m + 1))
                        act.wait_ge(zt_ready.sem, used(zt_ready, g, n, 4))
                        act.activation(z[:, n % 4, :, :].rearrange("p h e -> p (h e)"), mul_bank[m % 2][:, :], ACT.Tanh,
                                       scale=0.5).then_inc(tanh_done.sem, 1)
                    elif what == "Y":
                        act.wait_ge(y_ready.sem, y_ready.now(g, n + 1))
                        act.wait_ge(square_done.sem, used(square_done, g, n, 1))
                        for h in range(REP):
                            last = act.activation(junk[:, h, :], y_bank[:, h * D:(h + 1) * D], ACT.Square,
                                                  scale=(4.0 / D) ** 0.5, accum_out=sumsq[:, n, h:h + 1])
                        last.then_inc(square_done.sem, 1)
                    elif what == "T":
                        act.wait_ge(zt_ready.sem, zt_ready.now(g, n + 1))
                        o = mul_at("O", (n - 2) % NT) + 1
                        act.wait_ge(mul_ready.sem, mul_ready.now(g, o) if n >= 2 else mul_ready.last(g, o))
                        act.activation(z_hi[:, n % 2, :, :].rearrange("p h i -> p (h i)"), z_bank[:, :], ACT.Copy,
                                       scale=gnorm[:, 0:1]).then_inc(zhi_done.sem, 1)

        @block.vector
        def _(dve):
            for sg in (q_lo_done, cos_done, qk_lo_done, rot_done, silu_done, prob_done, z_done, zlo_done, x_added, head_copied):
                sg.start(dve)
            dve.wait_ge(table_loaded, 32)
            with dve.Fori(0, KVH) as g:
                for what, n in ORDER["vector"]:
                    if what == "H":
                        dve.wait_ge(decay_done.sem, decay_done.last(g, 3 * B))
                        dve.wait_ge(prob_done.sem, prob_done.last(g, 3 * B))
                        dve.tensor_copy(head[:, :, :], stats[:, :, ds(g * REP, REP)]).then_inc(head_copied.sem, 1)
                    elif what == "W":
                        dve.wait_ge(hi_done.sem, hi_done.now(g, 2))
                        dve.tensor_tensor(w["q"][1][:, :, :], raw_qo[:, :, :], w["q"][0][:, :, :].bitcast(F32),
                                          ALU.subtract).then_inc(q_lo_done.sem, 1)
                    elif what == "C":
                        dve.wait_ge(swap_done.sem, swap_done.now(g, n + 1))
                        dve.wait_ge(qk_lo_done.sem, used(qk_lo_done, g, n, 2))
                        dve.tensor_tensor(rot_a[:, n % 2, :], rot_bank[n % 2][:, :], cos,
                                          ALU.mult).then_inc(cos_done.sem, 1)
                    elif what == "A":
                        dve.wait_ge(sin_done.sem, sin_done.now(g, n + 1))
                        dve.wait_ge(cos_done.sem, cos_done.now(g, n + 1))
                        dve.tensor_tensor(rot_a[:, n % 2, :], rot_a[:, n % 2, :], rot_b[:, n % 2, :],
                                          ALU.add).then_inc(rot_done.sem, 1)
                    elif what == "L":
                        dve.wait_ge(qk_hi_done.sem, qk_hi_done.now(g, n + 1))
                        dve.tensor_tensor(rotated(1, n), rot_a[:, n % 2, :], rotated(0, n).bitcast(F32),
                                          ALU.subtract).then_inc(qk_lo_done.sem, 1)
                    elif what == "P":
                        b, (kc, qc) = n // 3, BLOCKS[n % 3]
                        dve.wait_ge(head_copied.sem, head_copied.now(g, 1))
                        dve.wait_ge(score_ready.sem, score_ready.now(g, n + 1))
                        dve.wait_ge(decay_done.sem, decay_done.now(g, n + 1))
                        for h in range(REP):
                            p = prob[:, b % 2, n % 3, h, :]
                            last = dve.scalar_tensor_tensor(out=p, in0=s_bank[n % 2][:, h * P:(h + 1) * P],
                                                            scalar=head[:, 2 * b + kc, h:h + 1], in1=p,
                                                            op0=ALU.mult, op1=ALU.mult)
                        last.then_inc(prob_done.sem, 1)
                    elif what == "G":
                        m = mul_at("G", n)
                        zt = z[:, n % 4, :, :].rearrange("p h e -> p (h e)")
                        dve.wait_ge(tanh_done.sem, tanh_done.now(g, n + 1))
                        dve.scalar_tensor_tensor(out=zt, in0=zt, scalar=1.0, in1=mul_bank[m % 2][:, :],
                                                 op0=ALU.add, op1=ALU.mult).then_inc(silu_done.sem, 1)
                    elif what == "Y":
                        dve.wait_ge(rinv_done.sem, rinv_done.now(g, n + 1))
                        dve.wait_ge(silu_done.sem, silu_done.now(g, n + 1))
                        for h in range(REP):
                            zt = z[:, n % 4, h, :]
                            last = dve.scalar_tensor_tensor(out=zt, in0=y_bank[:, h * D:(h + 1) * D],
                                                            scalar=rinv[:, n, h:h + 1], in1=zt,
                                                            op0=ALU.mult, op1=ALU.mult)
                        last.then_inc(z_done.sem, 1)
                    elif what == "T":
                        dve.wait_ge(zhi_done.sem, zhi_done.now(g, n + 1))
                        dve.scalar_tensor_tensor(out=z_lo[:, n % 2, :, :].rearrange("p h i -> p (h i)"),
                                                 in0=z_bank[:, :], scalar=gnorm[:, 0:1],
                                                 in1=z_hi[:, n % 2, :, :].rearrange("p h i -> p (h i)").bitcast(F32),
                                                 op0=ALU.mult, op1=ALU.subtract).then_inc(zlo_done.sem, 1)
                    elif what == "X":
                        m = mul_at("O", n)
                        dve.wait_ge(mul_ready.sem, mul_ready.now(g, m + 1))
                        dve.wait_ge(x_added.sem, x_added.last(g, n + 1))
                        dve.tensor_tensor(x[:, n, :], mul_bank[m % 2][:, :], x[:, n, :], ALU.add).then_inc(x_added.sem, 1)

        @block.tensor
        def _(pe):
            for sg in (rot_ready, mul_ready, score_ready, y_ready, zt_ready):
                sg.start(pe)

            def three_pass(out, a, b, k_range):
                for k in k_range:
                    for n, (i, j) in enumerate(((0, 0), (0, 1), (1, 0))):
                        last = pe.matmul(out, a(k)[i], b(k)[j], start=k == k_range[0] and n == 0,
                                         stop=k == k_range[-1] and n == 2)
                return last

            with pe.Fori(0, KVH) as g:

                def split_ready(n):
                    pe.wait_ge(hi_done.sem, hi_done.now(g, n + 1))
                    if n == 1:
                        pe.wait_ge(q_lo_done.sem, q_lo_done.now(g, 1))
                    else:
                        pe.wait_ge(lo_done.sem, lo_done.now(g, (1, None, 2, 3)[n]))

                def mul_free(m):
                    what, t = SHARED[(m - 2) % len(SHARED)]
                    sg = silu_done if what == "G" else x_added
                    pe.wait_ge(sg.sem, sg.now(g, t + 1) if m >= 2 else sg.last(g, t + 1))

                for what, n in ORDER["tensor"]:
                    if what == "R":
                        if n in (0, 2):
                            split_ready(0 if n == 0 else 1)
                        pe.wait_ge(cos_done.sem, used(cos_done, g, n, 2))
                        s, h = (n, 0) if n < 2 else ((n - 2) // REP, (n - 2) % REP)
                        wt, cols = w["k" if n < 2 else "q"], slice(s * HALF, (s + 1) * HALF)
                        three_pass(rot_bank[n % 2][:, :],
                                   lambda k: [m[:, k, h * D:(h + 1) * D] for m in wt],
                                   lambda k: (x_hi[:, k, cols], x_lo[:, k, cols]),
                                   range(KT)).then_inc(rot_ready.sem, 1)
                    elif what == "G":
                        if n == 0:
                            split_ready(2)
                        m = mul_at("G", n)
                        mul_free(m)
                        rows = slice(n * P, (n + 1) * P)
                        three_pass(mul_bank[m % 2][:, :], lambda k: (x_hi[:, k, rows], x_lo[:, k, rows]),
                                   lambda k: [a[:, k, :] for a in w["g"]], range(KT)).then_inc(mul_ready.sem, 1)
                    elif what == "S":
                        b, (kc, qc) = n // 3, BLOCKS[n % 3]
                        pe.wait_ge(qk_lo_done.sem, qk_lo_done.now(g, 2 + REP * (b // 2 + 1)))
                        pe.wait_ge(prob_done.sem, used(prob_done, g, n, 2))
                        keys = slice((2 * b + kc) * P, (2 * b + kc + 1) * P)
                        heads = slice(1 - b // 2, 1 - b // 2 + REP)
                        queries = slice((2 * (b % 2) + qc) * P, (2 * (b % 2) + qc + 1) * P)
                        three_pass(s_bank[n % 2][:, :], lambda k: (k_hi[:, keys], k_lo[:, keys]),
                                   lambda k: (q_hi[:, heads, queries], q_lo[:, heads, queries]),
                                   range(1)).then_inc(score_ready.sem, 1)
                    elif what == "Y":
                        b, qc = n // 2, n % 2
                        if n == 0:
                            pe.wait_ge(ld_v.sem, ld_v.now(g, 16))
                        pe.wait_ge(prob_done.sem, prob_done.now(g, 3 * b + (3 if qc else 1)))
                        pe.wait_ge(z_done.sem, used(z_done, g, n, 1))
                        mine = [(m, kc) for m, (kc, c) in enumerate(BLOCKS) if c == qc]
                        for h in range(REP):
                            for m, kc in mine:
                                last = pe.matmul(y_bank[:, h * D:(h + 1) * D], prob[:, b % 2, m, h, :],
                                                 v[:, 2 * b + kc, :], start=m == mine[0][0], stop=m == mine[-1][0])
                        last.then_inc(y_ready.sem, 1)
                    elif what == "T":
                        pe.wait_ge(z_done.sem, z_done.now(g, n + 1))
                        pe.wait_ge(zlo_done.sem, used(zlo_done, g, n, 1))
                        for h in range(REP):
                            last = pe.transpose(z_bank[:, h * P:(h + 1) * P], z[:, n % 4, h, :], ident[:, :])
                        last.then_inc(zt_ready.sem, 1)
                    elif what == "O":
                        if n == 0:
                            split_ready(3)
                        m = mul_at("O", n)
                        mul_free(m)
                        pe.wait_ge(zhi_done.sem, zhi_done.now(g, n + 1))
                        pe.wait_ge(zlo_done.sem, zlo_done.now(g, n + 1))
                        three_pass(mul_bank[m % 2][:, :], lambda h: (z_hi[:, n % 2, h, :], z_lo[:, n % 2, h, :]),
                                   lambda h: [a[:, h, :] for a in w["o"]], range(REP)).then_inc(mul_ready.sem, 1)


def build(nc, args, out):
    (x_in, w_q, w_k, w_v, w_g, w_o, w_in, dt_bias, a_log, gnorm, w_gate, w_up, w_down, squares, tables) = args
    with ExitStack() as ctx:
        sb = lambda n, s, d=F32: ctx.enter_context(nc.sbuf_tensor(n, s, d))
        x = sb("x", [P, NT, HID])
        ident, ones, out_scale = sb("ident", [P, P]), sb("ones", [P, P]), sb("out_scale", [P, 1])
        stats = sb("stats", [P, 2 * NT + B, H])
        ternary = [nc.dram_tensor(f"ternary{m}", [P, KT * FP], F16, kind="Internal").ap() for m in range(3)]
        v_dram = nc.dram_tensor("v_by_head", [KVH, P, NT, D], F32, kind="Internal").ap()
        g_dram = nc.dram_tensor("g_rows_dram", [H, TOK], F32, kind="Internal").ap()
        tiles = lambda a: a.rearrange("(t p) n -> p t n", p=P)
        place = Arena(nc, -(-nc.sbuf_base // 64) * 64)
        ctx.enter_context(nc.sbuf_tensor("arena", [P, ARENA // 4 + 16], F32))
        q = [place(f"q{m}", [P, KT, FP] if m < 2 else [P, FT, HID], F16, Q + m * 11 * KB) for m in range(3)]
        x_hi = place("ax_hi", [P, KT, TOK], F32R, AX_HI)
        x_lo = place("ax_lo", [P, KT, TOK], F32R, AX_LO)
        ins = AttentionInputs(ctx, nc, place, w_q, w_k, w_g, w_o, tables, gnorm)
        v_stored = [ctx.enter_context(nc.semaphore(f"v_stored{n}")) for n in range(4)]
        q_loaded = [ctx.enter_context(nc.semaphore(f"q{m}_loaded")) for m in range(3)]
        first_half(nc, place, x, tiles(x_in), x_hi, x_lo, stats, out_scale, ident, ones, q, (w_gate, w_up, w_down),
                   ternary, squares, w_v, w_in, dt_bias, a_log, v_dram, g_dram, ins.first_loads, v_stored)
        attention(nc, place, x, ident, x_hi, x_lo, stats, ins, v_dram, g_dram, v_stored, q, ternary, q_loaded)
        second_ffn(nc, place, x, out_scale, ident, ones, q, q_loaded, tiles(out))


def kernel(L0_attn_hidden_states, L0_attn_Wq, L0_attn_Wk, L0_attn_Wv, L0_attn_Wo, L0_attn_Wg, L0_attn_Win,
           L0_attn_dt_bias, L0_attn_A_log_bias, L0_attn_gnorm_w, L0_ffn_w_gate, L0_ffn_w_up, L0_ffn_w_down):
    import numpy as np
    import concourse.bacc as bacc
    from concourse.bass_utils import run_bass_kernel_spmd

    a = np.asarray
    by_head = lambda w: a(w).reshape(KVH, -1, KT, P).transpose(0, 3, 2, 1)
    contracted = lambda w: a(w).reshape(-1, KT, P).transpose(2, 1, 0)
    padded = np.zeros((FP - FF, HID), np.float32)
    inner_first = lambda w: np.concatenate([a(w), padded])
    gate, up = (contracted(inner_first(w)).reshape(P, KT * FP) for w in (L0_ffn_w_gate, L0_ffn_w_up))
    down = inner_first(a(L0_ffn_w_down).T).reshape(FT, P, HID).transpose(1, 0, 2).reshape(P, FT * HID)
    w_o = a(L0_attn_Wo).reshape(HID, KVH, REP, D).transpose(1, 3, 2, 0)

    i = np.arange(P)
    squares = np.stack([np.eye(P), i[:, None] <= i[None, :]], 1).astype(np.float32)
    inv_freq = (np.float32(1) / np.power(np.float32(10000), np.arange(0, D, 2, dtype=np.float32) / np.float32(D)))
    ang = (np.arange(L, dtype=np.float32)[:, None] * inv_freq.astype(np.float32)).astype(np.float64)
    cos = np.tile(np.concatenate([np.cos(ang), np.cos(ang)], 1).T, (1, HALF // L))
    sin = np.tile(np.concatenate([-np.sin(ang), np.sin(ang)], 1).T, (1, HALF // L))
    mask = np.tile(np.where(i[:, None] <= i[None, :], 0.0, -BIG), (1, REP))
    tables = np.stack([cos, sin, mask], 1).astype(np.float32)

    ins = {
        "x_in": a(L0_attn_hidden_states).reshape(TOK, HID),
        "w_q": by_head(L0_attn_Wq), "w_k": by_head(L0_attn_Wk), "w_v": contracted(L0_attn_Wv),
        "w_g": by_head(L0_attn_Wg), "w_o": w_o, "w_in": contracted(L0_attn_Win),
        "dt_bias": a(L0_attn_dt_bias).reshape(H, 1), "a_log": np.tile(a(L0_attn_A_log_bias), NT),
        "gnorm": a(L0_attn_gnorm_w).reshape(D, 1), "w_gate": gate, "w_up": up, "w_down": down,
        "squares": squares, "tables": tables,
    }
    nc = bacc.Bacc("TRN2", target_bir_lowering=False, num_devices=1)
    arrays, args = {}, []
    for name, v in ins.items():
        arrays[f"in_{name}"] = np.ascontiguousarray(v)
        args.append(nc.dram_tensor(f"in_{name}", arrays[f"in_{name}"].shape, mybir.dt.from_np(arrays[f"in_{name}"].dtype),
                                   kind="ExternalInput").ap())
    out = nc.dram_tensor("out", (TOK, HID), F32, kind="ExternalOutput").ap()
    build(nc, args, out)
    r = run_bass_kernel_spmd(nc, [arrays], core_ids=[0])
    return r.results[0]["out"].reshape(B, L, HID)
```
